# Optimizing a Trainium2 kernel written in Bass

```python
import numpy as np
import jax
import jax.numpy as jnp

def _softmax(x, axis=-1):
    return jax.nn.softmax(x, axis=axis)

def _gelu(x):
    return jax.nn.gelu(x, approximate=True)

def _silu(x):
    return jax.nn.silu(x)

def _sigmoid(x):
    return jax.nn.sigmoid(x)

def _layernorm(x, axis=-1, eps=1e-05):
    m = jnp.mean(x, axis=axis, keepdims=True)
    v = jnp.var(x, axis=axis, keepdims=True)
    return (x - m) / jnp.sqrt(v + eps)

def _scatter_add(tgt, idx, src, axis=0):
    return tgt.at[idx].add(src)

def _segment_sum(src, seg, n):
    return jax.ops.segment_sum(src, seg, n)
kernel_name = 'mk_metaformer_d2_conv_nchw512_r4_33ca97'

def setup_inputs(seed: int=0):
    np.random.seed(seed)
    _w = jnp.asarray

    def _rec_inputs():
        import jax
        import jax.numpy as jnp
        _gk = jax.random.key(seed)
        x = 7.22e-05 + 1 * jax.random.normal(jax.random.fold_in(_gk, 1), (16, 128, 32, 32), jnp.float32)
        return x
    x = _rec_inputs()

    def _L0_conv_setup():
        import jax, jax.numpy as jnp
        import numpy as np
        H = W = 32
        C = 128
        RED = 16

        def make_gus(v=1.5):
            idx = np.arange(H, dtype=np.float64)
            d2 = (idx[:, None] - idx[None, :]) ** 2
            g1 = np.exp(-d2 / (2.0 * v * v))
            g = np.einsum('ix,ky->ikxy', g1, g1) / (2.0 * np.pi * v * v)
            g = g / g.sum(axis=(2, 3), keepdims=True)
            return jnp.asarray(g.reshape(H * W, H, W), dtype=jnp.float32)

        def _patches3(img, h, w):
            ps = [img[:, :, dy:dy + h, dx:dx + w] for dy in range(3) for dx in range(3)]
            return jnp.stack(ps, axis=-1)
        key = jax.random.key(seed)
        ks = jax.random.split(key, 6)
        b = 16
        return {'x': jax.random.normal(ks[0], (b, C, H, W), dtype=jnp.float32), 'se_w1': jax.random.normal(ks[1], (C // RED, C), dtype=jnp.float32) * 0.02, 'se_b1': jnp.zeros((C // RED,), dtype=jnp.float32), 'se_w2': jax.random.normal(ks[2], (C, C // RED), dtype=jnp.float32) * 0.02, 'se_b2': jnp.zeros((C,), dtype=jnp.float32), 'down_w': jax.random.normal(ks[3], (C, 2 * C), dtype=jnp.float32) * 0.02, 'gus': make_gus(1.5)}
    _L0_conv_all = _L0_conv_setup()
    _L0_conv_in = {k: v for k, v in _L0_conv_all.items() if k in ('se_w1', 'se_b1', 'se_w2', 'se_b2', 'down_w', 'gus')}
    del _L0_conv_all

    def _L0_ffn_setup():
        import jax, jax.numpy as jnp
        import numpy as np
        NUM_EXPERTS = 8
        TOP_K = 2
        key = jax.random.key(seed)
        ks = jax.random.split(key, 6)
        B, S, D, F, E = (2, 512, 128, 384, NUM_EXPERTS)
        scale = 0.02
        return {'x': jax.random.normal(ks[0], (B, S, D), dtype=jnp.float32), 'Wg': jax.random.normal(ks[1], (D, E), dtype=jnp.float32) * scale, 'W1': jax.random.normal(ks[2], (E, D, F), dtype=jnp.float32) * scale, 'W2': jax.random.normal(ks[3], (E, F, D), dtype=jnp.float32) * scale, 'W3': jax.random.normal(ks[4], (E, D, F), dtype=jnp.float32) * scale, 'b3': jax.random.normal(ks[5], (E, F), dtype=jnp.float32) * scale}
    _L0_ffn_all = _L0_ffn_setup()
    _L0_ffn_in = {k: v for k, v in _L0_ffn_all.items() if k in ('Wg', 'W1', 'W2', 'W3', 'b3')}
    del _L0_ffn_all

    def _L1_conv_setup():
        import jax, jax.numpy as jnp
        import numpy as np
        from jax import lax
        DW_HASH_CH = 1337
        DW_HASH_KH = 7919
        DW_HASH_KW = 2971
        DW_HASH_LAYER = 104729
        SIGN_HASH_A = 4099
        SIGN_HASH_B = 6151
        SIGN_HASH_C = 14887
        CHANNELS = 128
        KH, KW = (7, 7)
        CODEBOOK_SIZE = 1024
        LAYER_ID = 3
        STRIDE = (1, 1)
        PADDING = ((3, 3), (3, 3))

        def _hash_tables():
            ch = np.arange(CHANNELS).reshape(CHANNELS, 1, 1)
            kh = np.arange(KH).reshape(1, KH, 1)
            kw = np.arange(KW).reshape(1, 1, KW)
            idx = (ch * DW_HASH_CH + kh * DW_HASH_KH + kw * DW_HASH_KW + LAYER_ID * DW_HASH_LAYER) % CODEBOOK_SIZE
            bits = (ch * SIGN_HASH_A + kh * SIGN_HASH_B + kw * SIGN_HASH_C + LAYER_ID * (SIGN_HASH_A + 29)) % 2
            signs = bits.astype(np.float32) * 2.0 - 1.0
            return (jnp.asarray(idx), jnp.asarray(signs))
        _IDX, _SIGNS = _hash_tables()
        key = jax.random.key(seed)
        k1, k2 = jax.random.split(key)
        x = jax.random.normal(k1, (16, CHANNELS, 24, 24), dtype=jnp.float32)
        codebook = jax.random.normal(k2, (CODEBOOK_SIZE,), dtype=jnp.float32) * 0.01
        bias = jnp.zeros((CHANNELS,), dtype=jnp.float32)
        return {'x': x, 'codebook': codebook, 'bias': bias}
    _L1_conv_all = _L1_conv_setup()
    _L1_conv_in = {k: v for k, v in _L1_conv_all.items() if k in ('codebook', 'bias')}
    del _L1_conv_all

    def _L1_ffn_setup():
        import jax, jax.numpy as jnp
        import numpy as np
        import math
        B, T, D = (4, 2048, 128)
        E, K, F = (8, 2, 512)
        CAP_FACTOR = 1.25
        key = jax.random.key(seed)
        ks = jax.random.split(key, 4)
        return {'x': jax.random.normal(ks[0], (B, T, D), jnp.float32), 'gate_w': jax.random.normal(ks[1], (E, D), jnp.float32) * 0.01, 'w1': jax.random.normal(ks[2], (E, D, F), jnp.float32) * (1.0 / np.sqrt(D)), 'b1': jnp.zeros((E, F), jnp.float32), 'w2': jax.random.normal(ks[3], (E, F, D), jnp.float32) * (1.0 / np.sqrt(F)), 'b2': jnp.zeros((E, D), jnp.float32)}
    _L1_ffn_all = _L1_ffn_setup()
    _L1_ffn_in = {k: v for k, v in _L1_ffn_all.items() if k in ('gate_w', 'w1', 'b1', 'w2', 'b2')}
    del _L1_ffn_all
    return {'x': x, 'L0_conv_se_w1': _L0_conv_in['se_w1'], 'L0_conv_se_b1': _L0_conv_in['se_b1'], 'L0_conv_se_w2': _L0_conv_in['se_w2'], 'L0_conv_se_b2': _L0_conv_in['se_b2'], 'L0_conv_down_w': _L0_conv_in['down_w'], 'L0_conv_gus': _L0_conv_in['gus'], 'L0_ffn_Wg': _L0_ffn_in['Wg'], 'L0_ffn_W1': _L0_ffn_in['W1'], 'L0_ffn_W2': _L0_ffn_in['W2'], 'L0_ffn_W3': _L0_ffn_in['W3'], 'L0_ffn_b3': _L0_ffn_in['b3'], 'L1_conv_codebook': _L1_conv_in['codebook'], 'L1_conv_bias': _L1_conv_in['bias'], 'L1_ffn_gate_w': _L1_ffn_in['gate_w'], 'L1_ffn_w1': _L1_ffn_in['w1'], 'L1_ffn_b1': _L1_ffn_in['b1'], 'L1_ffn_w2': _L1_ffn_in['w2'], 'L1_ffn_b2': _L1_ffn_in['b2']}

def reference(x, L0_conv_se_w1, L0_conv_se_b1, L0_conv_se_w2, L0_conv_se_b2, L0_conv_down_w, L0_conv_gus, L0_ffn_Wg, L0_ffn_W1, L0_ffn_W2, L0_ffn_W3, L0_ffn_b3, L1_conv_codebook, L1_conv_bias, L1_ffn_gate_w, L1_ffn_w1, L1_ffn_b1, L1_ffn_w2, L1_ffn_b2):
    import jax
    import jax.numpy as jnp

    def _L0_conv_ref(x, se_w1, se_b1, se_w2, se_b2, down_w, gus):
        import jax, jax.numpy as jnp
        import numpy as np
        H = W = 32
        C = 128
        RED = 16

        def make_gus(v=1.5):
            idx = np.arange(H, dtype=np.float64)
            d2 = (idx[:, None] - idx[None, :]) ** 2
            g1 = np.exp(-d2 / (2.0 * v * v))
            g = np.einsum('ix,ky->ikxy', g1, g1) / (2.0 * np.pi * v * v)
            g = g / g.sum(axis=(2, 3), keepdims=True)
            return jnp.asarray(g.reshape(H * W, H, W), dtype=jnp.float32)

        def _patches3(img, h, w):
            ps = [img[:, :, dy:dy + h, dx:dx + w] for dy in range(3) for dx in range(3)]
            return jnp.stack(ps, axis=-1)
        b, c, h, w = x.shape
        s = x.mean(axis=(2, 3))
        y = jax.nn.relu(s @ se_w1.T + se_b1)
        y = jax.nn.sigmoid(y @ se_w2.T + se_b2)
        out32 = x * y[:, :, None, None]
        gus_out = jnp.einsum('pyx,bcyx->bpc', gus, out32).reshape(b, c, h, w)
        sig = jax.nn.sigmoid(out32)
        sigp = _patches3(jnp.pad(sig, ((0, 0), (0, 0), (1, 1), (1, 1))), h, w)
        ffp = _patches3(jnp.pad(out32, ((0, 0), (0, 0), (1, 1), (1, 1))), h, w)
        logits = jnp.einsum('bcyx,bcyxk->byxk', sig, sigp) / c
        attn = jax.nn.softmax(logits, axis=-1)
        g2 = jnp.einsum('byxk,bcyxk->byxc', attn, ffp)
        out_csa = g2.reshape(b, c, h, w)
        cat = jnp.concatenate([gus_out, out_csa], axis=1)
        z = jnp.einsum('oi,biyx->boyx', down_w, cat)
        mu = z.mean(axis=(2, 3), keepdims=True)
        var = z.var(axis=(2, 3), keepdims=True)
        zn = (z - mu) * jax.lax.rsqrt(var + 1e-05)
        return jnp.where(zn >= 0, zn, 0.2 * zn)

    def _L0_ffn_ref(x, Wg, W1, W2, W3, b3):
        import jax, jax.numpy as jnp
        import numpy as np
        NUM_EXPERTS = 8
        TOP_K = 2
        logits = jnp.einsum('bsd,de->bse', x, Wg)
        top_logits, top_idx = jax.lax.top_k(logits, TOP_K)
        top_w = jax.nn.softmax(top_logits, axis=-1)
        onehot = jax.nn.one_hot(top_idx, NUM_EXPERTS, dtype=x.dtype)
        C = jnp.sum(onehot * top_w[..., None], axis=-2)
        h = jnp.einsum('bsd,edf->bsef', x, W1)
        g = jnp.einsum('bsd,edf->bsef', x, W3) + b3
        act = jax.nn.silu(h) * g
        out = jnp.einsum('bse,bsef,efd->bsd', C, act, W2)
        return out

    def _L1_conv_ref(x, codebook, bias):
        import jax, jax.numpy as jnp
        import numpy as np
        from jax import lax
        DW_HASH_CH = 1337
        DW_HASH_KH = 7919
        DW_HASH_KW = 2971
        DW_HASH_LAYER = 104729
        SIGN_HASH_A = 4099
        SIGN_HASH_B = 6151
        SIGN_HASH_C = 14887
        CHANNELS = 128
        KH, KW = (7, 7)
        CODEBOOK_SIZE = 1024
        LAYER_ID = 3
        STRIDE = (1, 1)
        PADDING = ((3, 3), (3, 3))

        def _hash_tables():
            ch = np.arange(CHANNELS).reshape(CHANNELS, 1, 1)
            kh = np.arange(KH).reshape(1, KH, 1)
            kw = np.arange(KW).reshape(1, 1, KW)
            idx = (ch * DW_HASH_CH + kh * DW_HASH_KH + kw * DW_HASH_KW + LAYER_ID * DW_HASH_LAYER) % CODEBOOK_SIZE
            bits = (ch * SIGN_HASH_A + kh * SIGN_HASH_B + kw * SIGN_HASH_C + LAYER_ID * (SIGN_HASH_A + 29)) % 2
            signs = bits.astype(np.float32) * 2.0 - 1.0
            return (jnp.asarray(idx), jnp.asarray(signs))
        _IDX, _SIGNS = _hash_tables()
        weight = codebook[_IDX] * _SIGNS.astype(codebook.dtype)
        weight = weight[:, None, :, :]
        out = lax.conv_general_dilated(x, weight, window_strides=STRIDE, padding=PADDING, dimension_numbers=('NCHW', 'OIHW', 'NCHW'), feature_group_count=CHANNELS)
        return out + bias[None, :, None, None]

    def _L1_ffn_ref(x, gate_w, w1, b1, w2, b2):
        import jax, jax.numpy as jnp
        import numpy as np
        import math
        B, T, D = (4, 2048, 128)
        E, K, F = (8, 2, 512)
        CAP_FACTOR = 1.25
        Bx, Tx, Dx = x.shape
        N = Bx * Tx
        C = math.ceil(CAP_FACTOR * N / E)
        xf = x.reshape(N, Dx)
        probs = jax.nn.softmax(xf @ gate_w.T, axis=-1)
        topk_vals, topk_idx = jax.lax.top_k(probs, K)
        topk_vals = topk_vals / topk_vals.sum(-1, keepdims=True)
        flat_e = topk_idx.reshape(N * K)
        onehot = jax.nn.one_hot(flat_e, E, dtype=jnp.int32)
        pos = jnp.cumsum(onehot, axis=0)[jnp.arange(N * K), flat_e] - 1
        keep = pos < C
        pos_safe = jnp.where(keep, pos, C)
        token_ids = jnp.repeat(jnp.arange(N), K)
        buf = jnp.zeros((E, C + 1, Dx), x.dtype).at[flat_e, pos_safe].set(xf[token_ids])
        expert_in = buf[:, :C]
        h = jax.nn.gelu(jnp.einsum('ecd,edf->ecf', expert_in, w1) + b1[:, None, :], approximate=False)
        expert_out = jnp.einsum('ecf,efd->ecd', h, w2) + b2[:, None, :]
        gathered = expert_out[flat_e, jnp.minimum(pos_safe, C - 1)]
        w = (topk_vals.reshape(N * K) * keep).astype(x.dtype)
        out = (gathered * w[:, None]).reshape(N, K, Dx).sum(axis=1)
        return out.reshape(Bx, Tx, Dx)

    def _gn(v, G=32, eps=1e-05):
        B_, C_, H_, W_ = v.shape
        g = v.reshape(B_, G, C_ // G, H_, W_)
        m = jnp.mean(g, axis=(2, 3, 4), keepdims=True)
        s = jnp.var(g, axis=(2, 3, 4), keepdims=True)
        return ((g - m) / jnp.sqrt(s + eps)).reshape(v.shape)

    def _ln_c(v, eps=1e-06):
        m = jnp.mean(v, axis=1, keepdims=True)
        s = jnp.var(v, axis=1, keepdims=True)
        return (v - m) / jnp.sqrt(s + eps)

    def _ln_t(v, eps=1e-05):
        m = jnp.mean(v, axis=-1, keepdims=True)
        s = jnp.var(v, axis=-1, keepdims=True)
        return (v - m) / jnp.sqrt(s + eps)

    def _to_tokens(v):
        B_, C_, H_, W_ = v.shape
        return v.reshape(B_, C_, H_ * W_).transpose(0, 2, 1)

    def _from_tokens(t, like):
        B_, C_, H_, W_ = like.shape
        return t.transpose(0, 2, 1).reshape(B_, C_, H_, W_)
    x = x + _L0_conv_ref(_ln_c(x), L0_conv_se_w1, L0_conv_se_b1, L0_conv_se_w2, L0_conv_se_b2, L0_conv_down_w, L0_conv_gus)
    t = _to_tokens(x)
    t = t + _L0_ffn_ref(_ln_t(t), L0_ffn_Wg, L0_ffn_W1, L0_ffn_W2, L0_ffn_W3, L0_ffn_b3)
    x = _from_tokens(t, x)
    x = x + _L1_conv_ref(_ln_c(x), L1_conv_codebook, L1_conv_bias)
    t = _to_tokens(x)
    t = t + _L1_ffn_ref(_ln_t(t), L1_ffn_gate_w, L1_ffn_w1, L1_ffn_b1, L1_ffn_w2, L1_ffn_b2)
    x = _from_tokens(t, x)
    return x

_drawn_inputs = setup_inputs


def setup_inputs(seed=0):
    import zlib

    import numpy as np

    out = dict(_drawn_inputs(seed))
    spreads = {'L0_conv_se_b1': (0.0, 0.8),
     'L0_conv_se_b2': (0.0, 0.1),
     'L1_conv_bias': (0.0, 0.1),
     'L1_ffn_b1': (0.0, 0.27),
     'L1_ffn_b2': (0.0, 0.1)}
    factors = {'L0_conv_se_w1': 24.281, 'L0_conv_se_w2': 7.394, 'L0_ffn_b3': 20.64}
    for name, (base, spread) in spreads.items():
        noise = np.random.default_rng([zlib.crc32(name.encode()), seed]).standard_normal(out[name].shape)
        drawn = base * np.exp(spread * noise) if base else spread * noise
        out[name] = jnp.asarray(drawn.astype(out[name].dtype))
    for name, factor in factors.items():
        out[name] = (out[name] * factor).astype(out[name].dtype)
    return out
```

```python
from contextlib import ExitStack

import concourse.bass as bass
from concourse import mybir

F32 = mybir.dt.float32
I32 = mybir.dt.int32
U32 = mybir.dt.uint32
ALU = mybir.AluOpType
ACT = mybir.ActivationFunctionType
AX_X = mybir.AxisListType.X
P = 128


class Order:

    def __init__(self, eng, sem, visit, per):
        self.eng, self.sem, self.base, self.per, self.k = eng, sem, visit * per, per, 0

    def step(self, ins):
        ins.then_inc(self.sem, 1)
        self.k += 1

    def settle(self):
        self.eng.wait_ge(self.sem, self.base + self.k)

    def link(self, ins):
        self.step(ins)
        self.settle()

    def end(self):
        assert self.k == self.per, (self.sem, self.k, self.per)


RSQRT_LINKS = 10


def rsqrt(v, order, x, y_int, tmp, out_ins):
    order.link(v.tensor_scalar(y_int, x.bitcast(I32), 1, None, ALU.arith_shift_right))
    order.link(v.tensor_scalar(y_int, y_int, -1, 0x5F3759DF, ALU.mult, ALU.add))
    y = y_int.bitcast(F32)
    for n in range(3):
        order.link(v.scalar_tensor_tensor(out=tmp, in0=y, scalar=-0.5, in1=y, op0=ALU.mult, op1=ALU.mult))
        order.link(v.tensor_tensor(tmp, tmp, x, ALU.mult))
        if n < 2:
            order.link(v.scalar_tensor_tensor(out=y, in0=tmp, scalar=1.5, in1=y, op0=ALU.add, op1=ALU.mult))
    return out_ins(tmp, y)


class Arena:

    def __init__(self, tensor, words):
        self.tensor, self.words, self.at = tensor, words, 0

    def take(self, *shape, parts=P):
        n = 1
        for s in shape:
            n *= s
        ap = self.tensor[0:parts, self.at:self.at + n]
        self.at += n
        assert self.at <= self.words, ("SBUF is full", self.at, self.words)
        if len(shape) == 2:
            ap = ap.rearrange("p (a b) -> p a b", a=shape[0])
        elif len(shape) == 3:
            ap = ap.rearrange("p (a b c) -> p a b c", a=shape[0], b=shape[1])
        return ap


def repeat(eng, first, last, body):
    body(first)
    with eng.Fori(first + 1, last) as turn:
        body(turn)


STAT_LINKS = 7


def token_stats(v, order, st, mean, var, tmp, eps, n):
    even, odd, even2, odd2 = (st[:, 0:n, c] for c in (1, 4, 2, 5))
    order.step(v.tensor_tensor(mean, even, odd, ALU.add))
    order.step(v.tensor_tensor(tmp, even, odd, ALU.subtract))
    order.link(v.tensor_tensor(var, even2, odd2, ALU.add))
    order.step(v.tensor_scalar(mean, mean, 0.5, None, ALU.mult))
    order.link(v.tensor_tensor(tmp, tmp, tmp, ALU.mult))
    order.link(v.scalar_tensor_tensor(out=var, in0=tmp, scalar=P / 4, in1=var, op0=ALU.mult, op1=ALU.add))
    order.link(v.tensor_scalar(var, var, 1.0 / P, eps, ALU.mult, ALU.add))


B, C, HW = 16, 128, 1024
IMG = 32
NBLK = B * HW // P
KB = HW // P
PAIRS = B // 2
E8 = 8
WIN = 6 * IMG
XS_W = 132
HALO = HW + 2 * IMG

GROUPS = 2
GB = NBLK // GROUPS
F0 = 384
FC0 = F0 // P
RING = 8
TILES0 = -(-(2 * GB + E8 - 1) // RING) * RING
F1 = 512
FC1 = F1 // P
CAP = -(-5 * B * HW // (4 * E8))
CT = CAP // P
assert CT * P == CAP
QT = 4
ROW_W = 132
NOWHERE = 1 << 20
TOKENS = B * HW
KER = 7
CODES = 1024
CG = 8
NCG = C // CG
EDGE = KER // 2
DX = 2 * IMG - 1


def code_place(kh, kw):
    inverse = pow(1337 % CODES, -1, CODES)
    return (kh * 7919 + kw * 2971 + 3 * 104729) * inverse % CODES


def metaformer(nc, x, se_w1, se_b1, se_w2, se_b2, down_w, gus, moe_wg, moe_w1, moe_w2, moe_w3, moe_b3,
               codebook, conv_bias, gate_w, ffn_w1, ffn_b1, ffn_w2, ffn_b2, out):
    hid = se_w1.shape[0]
    with ExitStack() as ctx:
        sems = {}

        def sem(name):
            if name not in sems:
                sems[name] = ctx.enter_context(nc.semaphore(name))
            return sems[name]

        WORDS = 53200
        arena = Arena(ctx.enter_context(nc.sbuf_tensor("arena", [P, WORDS], F32)), WORDS)
        tp = [ctx.enter_context(nc.psum_tensor(f"tp{i}", [P, 1024], F32)) for i in range(2)]
        zp = [ctx.enter_context(nc.psum_tensor(f"zp{i}", [P, 512], F32)) for i in range(2)]
        gp = [ctx.enter_context(nc.psum_tensor(f"gp{i}", [P, 512], F32)) for i in range(2)]

        xt = arena.take(NBLK, P)
        idle = arena.take(2)
        ident = arena.take(P)
        ones = arena.take(P)
        upper = arena.take(P)
        logits = arena.take(NBLK, E8)
        ln_mean = arena.take(NBLK)
        ln_rstd = arena.take(NBLK)
        ln_var = arena.take(16)
        rs_int = arena.take(16)
        rs_tmp = arena.take(16)
        moe_wg_s = arena.take(E8)
        gate_s = arena.take(E8)
        prefer = arena.take(E8)
        cap_base = arena.take(E8)
        carry = arena.take(E8)
        taken = arena.take(E8)
        n_tiles = arena.take(E8)
        first_slot = arena.take(E8)
        tile_no = arena.take(TILES0)
        tile_expert = [arena.take(TILES0) for _ in range(GROUPS)]
        slot = arena.take(2, NBLK)
        weight = arena.take(2, NBLK)
        row_id = arena.take(2, NBLK)
        fill = arena.take(ROW_W)
        piece = arena.take(4, ROW_W)
        piece_slot = arena.take(4)
        routing = arena.at
        top = arena.take(4, GB)
        e_hot = arena.take(2, GB, E8)
        e_tmp = arena.take(3, GB, E8)
        phase = arena.at
        wg = arena.take(8, KB, P)
        w2t = arena.take(P)
        mask = arena.take(6, IMG)
        npad = arena.take(KB)
        w1t_se = arena.take(hid)
        w2t_se = arena.take(P)
        b1_se = arena.take(1)
        b2_se = arena.take(1)
        hidden = arena.take(2)
        xsum = arena.take(2)
        gatey = arena.take(2)
        xs = [arena.take(2, KB, XS_W) for _ in range(2)]
        xc = arena.take(2, HW)
        sig = arena.take(2, HALO)
        ee = arena.take(KB, WIN)
        g2n = arena.take(KB, P)
        g2r = [arena.take(2, 8, P) for _ in range(2)]
        zz = [arena.take(2, HW) for _ in range(2)]
        xr = arena.take(HW)
        tn = arena.take(KB, P)
        tnc = xr.rearrange("p (k c) -> p k c", k=KB)
        st = arena.take(16, 6)
        mean_f = arena.take(16)
        rstd_f = arena.take(16)
        zst = arena.take(4, 6)
        zmv = arena.take(2, 2)
        zsc = arena.take(2)
        znm = arena.take(2)
        rden = arena.take(KB)
        t32 = arena.take(8)
        half_xn = NBLK // 2 * P
        arena.at = phase + half_xn
        m1_s = arena.take(E8 * F0)
        m3_s = arena.take(E8 * F0)
        m2_s = arena.take(E8, FC0, P)
        b3_s = arena.take(E8 * F0)
        tile_in = [arena.take(ROW_W) for _ in range(RING)]
        tok_t = [arena.take(P) for _ in range(2)]
        act_h = [arena.take(F0) for _ in range(2)]
        act_g = [arena.take(F0) for _ in range(2)]
        act_t = [arena.take(FC0, P) for _ in range(2)]
        y_tile = [arena.take(P) for _ in range(RING)]
        mean_c = [arena.take(KB // 2) for _ in range(2)]
        rstd_c = [arena.take(KB // 2) for _ in range(2)]
        var_c = arena.take(KB)
        st_c = arena.take(KB, 6)
        rsi_c = arena.take(KB)
        rst_c = arena.take(KB)
        toep = [arena.take(12, IMG, CG)]
        conv_b = arena.take(P)
        arena.at = phase
        xn = arena.take(NBLK, P)
        toep.append(arena.take(12, IMG, CG))
        arena.at = routing
        y_in = [arena.take(KB // 2, 2, P) for _ in range(2)]
        arena.at = phase
        tn4 = [arena.take(KB, P) for _ in range(2)]
        tnc4 = [arena.take(KB, P) for _ in range(2)]
        fw1 = [arena.take(F1) for _ in range(2)]
        fw2 = [arena.take(FC1, P) for _ in range(2)]
        fb1 = [arena.take(FC1) for _ in range(2)]
        fb2 = [arena.take(P) for _ in range(2)]
        quad_in = [arena.take(QT, ROW_W) for _ in range(CT // QT)]
        quad_t = [arena.take(QT * P) for _ in range(2)]
        hid_t = [arena.take(FC1, QT * P) for _ in range(2)]
        y_quad = [arena.take(QT, P) for _ in range(2)]
        y_fin = [arena.take(KB // 2, 2, P) for _ in range(2)]
        fin = [arena.take(KB // 2, P) for _ in range(2)]
        fin_t = [arena.take(KB // 2 * P) for _ in range(2)]
        var_r = arena.take(KB)
        st_r = arena.take(KB, 6)
        rsi_r = arena.take(KB)
        rst_r = arena.take(KB)

        def scratch(name, *shape):
            return nc.dram_tensor(name, shape, F32, kind="Internal").ap()

        slots = [scratch(f"slots_{g}", TILES0 * P, ROW_W) for g in range(GROUPS)] + [scratch("slots_cap", E8 * CAP, ROW_W)]
        results = scratch("results", 2 * TOKENS, P)
        codes = scratch("codes", CODES + P)
        by_dist = scratch("by_dist", NCG, KER, DX, CG)
        taps = scratch("taps", NCG, IMG, KER, IMG, CG)
        code_idx = piece[:, 0, 0:8]
        code_val = piece[:, 0, 8:16]
        tap_w = piece[0:KER * KER, 1, 0:P]
        tap_sign = piece[0:KER * KER, 2, 0:P]
        gus_s = xt[:, 0:8 * KB, :].rearrange("p (j k) c -> p j (k c)", j=8)
        dw_s = xt[:, 64:66, :].rearrange("p a b -> p (a b)")
        w1t = xt[:, 66, :]

        banks = [tp[0][:, 0:512], tp[0][:, 512:1024], tp[1][:, 0:512], tp[1][:, 512:1024],
                 zp[0][:, :], zp[1][:, :], gp[0][:, :], gp[1][:, :]]

        block = ctx.enter_context(nc.Block())

        def pipeline(eng, visit, route=None, aside=None):
            visit(0, 0, True, False, False)
            if aside is not None:
                aside(0)
            visit(1, 1, True, True, False)
            if aside is not None:
                aside(1)
            with eng.Fori(1, 3) as turn:
                visit(2 * turn, 0, True, True, True)
                visit(2 * turn + 1, 1, True, True, True)
            if route is not None:
                route(0)
            visit(6, 0, True, True, True)
            visit(7, 1, True, True, True)
            visit(PAIRS, 0, False, True, True)
            visit(PAIRS + 1, 1, False, False, True)
            if route is not None:
                route(1)

        @block.sync
        def _(sp):
            ld = lambda dst, src: sp.dma_start(dst, src, allow_slow_non_contiguous=True).then_inc(sem("const_in"), 16)
            sp.dma_start(xc, x[0:2].rearrange("b c p -> c b p")).then_inc(sem("x_in"), 16)
            ld(dw_s, down_w)
            sp.dma_start(gus_s, gus.rearrange("(a j) q -> a j q", j=8)).then_inc(sem("gus_in"), 16)
            ld(w1t_se, se_w1.rearrange("h c -> c h"))
            ld(w2t_se[0:hid, :], se_w2.rearrange("c h -> h c"))
            ld(b1_se[0:hid, :], se_b1.rearrange("(h a) -> h a", a=1))
            ld(b2_se, se_b2.rearrange("(h a) -> h a", a=1))
            ld(moe_wg_s, moe_wg)

            ld(gate_s, gate_w.rearrange("e c -> c e"))
            def aside(n):
                if n == 0:
                    sp.wait_ge(sem("pool_const"), 1)
                    sp.dma_start(by_dist.rearrange("g y x c -> (g y x c)").rearrange("(p a w) -> p a w", p=P, a=KER),
                                 fill[:, 0:DX].rearrange("p (a w) -> p a w", a=1).to_broadcast([P, KER, DX])
                                 ).then_inc(sem("taps_zero"), 16)
                    sp.wait_ge(sem("codes_in"), 16 * (CODES // P))
                    sp.dma_start(codes[0:CODES].rearrange("(a p) -> p a", p=P), code_val, allow_slow_non_contiguous=True
                                 ).then_inc(sem("codes_out"), 16)
                    sp.dma_start(codes[CODES:CODES + P].rearrange("(p a) -> p a", a=1), code_val[:, 0:1],
                                 allow_slow_non_contiguous=True).then_inc(sem("codes_out"), 16)
                    sp.wait_ge(sem("codes_out"), 32)
                    for row in range(KER * KER):
                        at = code_place(KER - 1 - row // KER, KER - 1 - row % KER)
                        sp.dma_start(tap_w[row:row + 1, :], codes[at:at + P].rearrange("(a c) -> a c", a=1)
                                     ).then_inc(sem("tapw_in"), 16)
                else:
                    sp.wait_ge(sem("tapw_ready"), 1)
                    sp.wait_ge(sem("taps_zero"), 16)
                    for dy in range(KER):
                        sp.dma_start(by_dist[:, dy, IMG - 1 - EDGE:IMG + EDGE, :].rearrange("g x c -> x g c"),
                                     tap_w[KER * dy:KER * dy + KER, :].rearrange("p (g c) -> p g c", c=CG)
                                     ).then_inc(sem("dist_out"), 16)

            def fill_slots(m, first, rows):
                sp.dma_start(slots[m].rearrange("(p r) w -> p r w", p=P)[:, bass.ds(first, rows), :],
                             fill.rearrange("p (a w) -> p a w", a=1).to_broadcast([P, rows, ROW_W])
                             ).then_inc(sem(f"fill_out{m}"), 16)

            def visit(i, s, front, mid, back):
                if back:
                    for b in range(2):
                        if b:
                            sp.wait_ge(sem("x1_ready"), 2 * (i - 2) + 1)
                        sp.dma_start(xr, x[bass.ds(2 * (i - 2) + b, 1)].rearrange("b c p -> c (b p)")
                                     ).then_inc(sem("res_in"), 16)
                if front and not (isinstance(i, int) and i == PAIRS - 1):
                    sp.wait_ge(sem("f1_done"), 2 * i + 2)
                    sp.dma_start(xc, x[bass.ds(2 * i + 2, 2)].rearrange("b c p -> c b p")).then_inc(sem("x_in"), 16)
                if front:
                    for b in range(2):
                        for k in range(KB):
                            sp.wait_ge(sem("g2_ready"), 4 * (2 * i + b) + k // 2 + 1)
                            sp.dma_start(g2r[s][16 * k:16 * k + 16, b].rearrange("a j c -> a j c"), g2n[:, k, :]
                                         ).then_inc(sem("g2r_in"), 16)
                if back:
                    sp.wait_ge(sem("x1_ready"), 2 * (i - 2) + 2)
                    sp.wait_ge(sem("lg_done"), 2 * (i - 2) + 2)
                    m = int(isinstance(i, int))
                    fill_slots(m, (i - 2 - 4 * m) * (TILES0 // 4), TILES0 // 4)

            pipeline(sp, visit, aside=aside)

            sp.wait_ge(sem("z_ready"), 8 * PAIRS)
            sp.wait_ge(sem("lg_ready"), PAIRS)
            for dst, src in ((m1_s.rearrange("p (e f) -> p e f", e=E8), moe_w1.rearrange("e d f -> d e f")),
                             (m3_s.rearrange("p (e f) -> p e f", e=E8), moe_w3.rearrange("e d f -> d e f")),
                             (m2_s, moe_w2.rearrange("e (c f) d -> f e c d", f=P)),
                             (b3_s, moe_b3.rearrange("(a e) f -> a (e f)", a=1).partition_broadcast(P))):
                sp.dma_start(dst, src).then_inc(sem("moe_in"), 16)
            sp.wait_ge(sem("dist_out"), 16 * KER)
            for col in range(IMG):
                sp.dma_start(taps[:, col].rearrange("g y x c -> g y (x c)"),
                             by_dist[:, :, IMG - 1 - col:DX - col, :].rearrange("g y x c -> g y (x c)")
                             ).then_inc(sem("taps_out"), 16)
            turns = TILES0 // RING

            def load_tiles(g, turn):
                for q in range(RING):
                    sp.wait_ge(sem(f"y_out{q}"), 16 * (g * turns + turn))
                    sp.dma_start(tile_in[q], slots[g][bass.ds((turn * RING + q) * P, P), :]
                                 ).then_inc(sem(f"tile_in{q}"), 16)

            rows = E8 * CT // (turns - 1)
            by_token = results.rearrange("(k p s) c -> p k (s c)", p=P, s=2)

            def load_results(dst, name, n, u):
                sp.dma_start(dst[u].rearrange("p k s c -> p k (s c)"), by_token[:, bass.ds(4 * n, 4), :]
                             ).then_inc(sem(f"{name}{u}"), 16)

            def load_toep(g):
                if g >= 2:
                    sp.wait_ge(sem("conv_done"), CG // 4 * (g - 1))
                for y in range(4):
                    src = taps[g].rearrange("i a x c -> i a (x c)")
                    sp.dma_start(toep[g % 2][IMG * y:IMG * y + IMG, y + 1:y + 1 + KER].rearrange("p a x c -> p a (x c)"), src
                                 ).then_inc(sem(f"toep_in{g % 2}"), 16)

            for q in range(4):
                sp.wait_ge(sem(f"piece_out{q}"), 16 * (GB // 2))
            repeat(sp, 0, turns, lambda turn: load_tiles(0, turn))
            for q in range(4):
                sp.wait_ge(sem(f"piece_out{q}"), 16 * (GB // 2) * 2)
            sp.dma_start(conv_b, conv_bias.rearrange("(a c) -> a c", a=1).partition_broadcast(P)).then_inc(sem("convb_in"), 16)
            sp.wait_ge(sem("taps_out"), 16 * IMG)
            sp.wait_ge(sem("toep_zero"), 1)
            load_toep(0)
            sp.wait_ge(sem("weighed"), 2)

            def beside(turn, u):
                load_tiles(1, turn)
                if isinstance(turn, int):
                    if turn == 0:
                        for q in range(RING):
                            sp.wait_ge(sem(f"y_out{q}"), 16 * turns)
                else:
                    sp.wait_ge(sem("x2_ready"), turn - 1)
                load_results(y_in, "y_in", turn, u)
                fill_slots(2, rows * turn, rows)

            for u in range(2):
                beside(u, u)
            with sp.Fori(1, turns // 2) as turn:
                for u in range(2):
                    beside(2 * turn + u, u)
            load_tiles(1, turns - 1)

            for q in range(RING):
                sp.wait_ge(sem(f"y_out{q}"), 16 * turns * GROUPS)
            with sp.Fori(NBLK // 16, NBLK // 8) as turn:
                for u in range(2):
                    sp.wait_ge(sem("x2_ready"), 2 * turn + u - 1)
                    load_results(y_in, "y_in", 2 * turn + u, u)
            sp.wait_ge(sem("toep_zero"), 2)
            load_toep(1)
            for g in range(2, NCG):
                load_toep(g)

            sp.wait_ge(sem("x3_ready"), C // 4)

            def load_expert(e, s):
                for dst, src in ((fw1[s], ffn_w1[bass.ds(e, 1)].rearrange("e d f -> d (e f)")),
                                 (fw2[s], ffn_w2[bass.ds(e, 1)].rearrange("e (c f) d -> f (e c) d", f=P)),
                                 (fb1[s], ffn_b1[bass.ds(e, 1)].rearrange("e (c f) -> f (e c)", f=P)),
                                 (fb2[s], ffn_b2[bass.ds(e, 1)].partition_broadcast(P))):
                    sp.dma_start(dst, src, allow_slow_non_contiguous=True).then_inc(sem(f"expert_in{s}"), 16)

            load_expert(0, 0)
            load_expert(1, 1)
            for q in range(4):
                sp.wait_ge(sem(f"piece_out{q}"), 16 * (GB // 2) * 4)
            per = CT // QT

            def load_quads(pair, s):
                for m in range(per):
                    sp.wait_ge(sem(f"yq_out{m}"), 64 * (2 * pair + s))
                    sp.dma_start(quad_in[m], slots[2][bass.ds((2 * per * pair + per * s + m) * QT * P, QT * P), :]
                                 .rearrange("(q p) w -> p q w", p=P)).then_inc(sem(f"quad_in{m}"), 16)

            load_quads(0, 0)
            load_quads(0, 1)
            with sp.Fori(1, E8 // 2) as pair:
                for s in range(2):
                    sp.wait_ge(sem("yq_ready"), per * (2 * pair - 1 + s))
                    load_expert(2 * pair + s, s)
                    load_quads(pair, s)

            for m in range(per):
                sp.wait_ge(sem(f"yq_out{m}"), 64 * E8)
            for u in range(2):
                load_results(y_fin, "yf_in", u, u)
            with sp.Fori(1, NBLK // 8) as turn:
                for u in range(2):
                    sp.wait_ge(sem("fin_ready"), 2 * turn + u - 1)
                    load_results(y_fin, "yf_in", 2 * turn + u, u)

        @block.gpsimd
        def _(pool):
            g = nc.gpsimd
            n = [0]

            def link(ins):
                n[0] += 1
                ins.then_inc(sem("pool_own"), 1)
                pool.wait_ge(sem("pool_own"), n[0])

            g.memset(ident, 0.0)
            g.memset(idle, 0.0)
            g.memset(ones, 1.0)
            g.memset(fill, 0.0)
            g.memset(carry, 0.0)
            link(g.memset(piece.rearrange("p a b -> p (a b)"), 0.0))
            link(g.iota(code_idx.bitcast(I32), pattern=[[P * 1337 % CODES, 8]], base=0, channel_multiplier=1337 % CODES))
            g.iota(fill[:, P:P + 1].bitcast(I32), pattern=[[0, 1]], base=NOWHERE, channel_multiplier=0)
            for k in range(2):
                g.iota(row_id[:, k, :].bitcast(I32), pattern=[[2 * P, NBLK]], base=k, channel_multiplier=2)
            exact = dict(allow_small_or_imprecise_dtypes=True)
            g.iota(prefer, pattern=[[-1, E8]], base=E8, channel_multiplier=0, **exact)
            g.iota(cap_base, pattern=[[CAP, E8]], base=0, channel_multiplier=0, **exact)
            g.iota(tile_no, pattern=[[1, TILES0]], base=0, channel_multiplier=0, **exact)
            link(g.iota(tap_sign.bitcast(I32), pattern=[[1, P]], base=0, channel_multiplier=1))
            g.memset(t32[:, 6:7], 0.0).then_inc(sem("iotas"), 1)
            g.memset(mask.rearrange("p a b -> p (a b)"), 0.0)
            g.memset(npad, 3.0)
            for s in range(2):
                g.memset(xs[s][:, :, :, P:P + 1], 1.0)
            g.memset(sig[:, :, 0:IMG], 0.0)
            link(g.memset(sig[:, :, HALO - IMG:HALO], 0.0))
            link(g.affine_select(out=ident, in_=ident, compare_op=ALU.not_equal, fill=1.0, base=0,
                                 pattern=[[-1, P]], channel_multiplier=1))
            link(g.affine_select(out=upper, in_=ones, compare_op=ALU.is_gt, fill=0.0, base=0,
                                 pattern=[[1, P]], channel_multiplier=-1))
            for y in range(4):
                band = mask[IMG * y:IMG * y + IMG, y:y + 3, :]
                one = ones[IMG * y:IMG * y + IMG, 0:96].rearrange("p (a b) -> p a b", a=3)
                link(g.affine_select(out=band, in_=one, compare_op=ALU.is_ge, fill=0.0, base=1,
                                     pattern=[[0, 3], [-1, IMG]], channel_multiplier=1))
                link(g.affine_select(out=band, in_=band, compare_op=ALU.is_ge, fill=0.0, base=1,
                                     pattern=[[0, 3], [1, IMG]], channel_multiplier=-1))
            g.memset(npad[0:IMG, 0:1], 2.0)
            link(g.memset(npad[P - IMG:P, KB - 1:KB], 2.0))
            link(g.iota(t32[:, 0:1].bitcast(I32), pattern=[[0, 1]], base=0, channel_multiplier=1))
            g.memset(t32[:, 4:5], 0.0).then_inc(sem("pool_const"), 1)
            pool.wait_ge(sem("code_idx"), 1)
            for a in range(CODES // P):
                g.indirect_dma_start(code_val[:, a:a + 1], None, codebook.rearrange("(n a) -> n a", a=1),
                                     bass.IndirectOffsetOnAxis(ap=code_idx[:, a:a + 1].bitcast(U32), axis=0),
                                     bounds_check=CODES - 1, oob_is_err=False).then_inc(sem("codes_in"), 16)

            def alone(name, count):
                pool.wait_ge(sem(name), count)
                if not isinstance(count, int):
                    pool.sem_inc(sem("passed"), 1)

            def send(r, q, turn):
                g.indirect_dma_start(slots[min(r, 2)], bass.IndirectOffsetOnAxis(ap=piece_slot[:, q:q + 1].bitcast(U32), axis=0),
                                     piece[:, q, :], None, bounds_check=slots[min(r, 2)].shape[0] - 1, oob_is_err=False
                                     ).then_inc(sem(f"piece_out{q}"), 16)

            pool.wait_ge(sem("fill_out0"), 16 * 4)
            pool.wait_ge(sem("dist_out"), 16 * KER)
            pool.wait_ge(sem("slots_ready"), 1)

            def first_rows(turn):
                for u in range(2):
                    blk = 2 * turn + u
                    for k in range(2):
                        q = 2 * u + k
                        if not isinstance(turn, int):
                            alone(f"piece_out{q}", 16 * turn)
                        row = piece[:, q, 0:P]
                        if k == 0:
                            g.tensor_tensor(row, xt[:, bass.ds(blk, 1), :].rearrange("p a c -> p (a c)"),
                                            ln_mean[:, bass.ds(blk, 1)].to_broadcast([P, P]), ALU.subtract
                                            ).then_inc(sem(f"centred{q}"), 1)
                            pool.wait_ge(sem(f"centred{q}"), turn + 1)
                            g.tensor_tensor(row, row, ln_rstd[:, bass.ds(blk, 1)].to_broadcast([P, P]), ALU.mult
                                            ).then_inc(sem(f"row_own{q}"), 1)
                            pool.wait_ge(sem(f"row_own{q}"), turn + 1)
                        else:
                            g.tensor_copy(row, piece[:, q - 1, 0:P])
                        g.tensor_copy(piece[:, q, P:P + 1].bitcast(I32), row_id[:, k, bass.ds(blk, 1)].bitcast(I32))
                        g.tensor_copy(piece_slot[:, q:q + 1].bitcast(I32), slot[:, k, bass.ds(blk, 1)].bitcast(I32)
                                      ).then_inc(sem(f"piece_made{q}"), 1)
                        alone(f"piece_made{q}", turn + 1)
                        send(0, q, turn)

            repeat(pool, 0, GB // 2, first_rows)

            def result_out(visit, q):
                alone("y_ready", RING * visit + q + 1)
                g.indirect_dma_start(results, bass.IndirectOffsetOnAxis(ap=tile_in[q][:, P:P + 1].bitcast(U32), axis=0),
                                     y_tile[q], None, bounds_check=2 * TOKENS - 1, oob_is_err=False
                                     ).then_inc(sem(f"y_out{q}"), 16)

            def piece_out(r, turn, q):
                alone(f"piece_made{q}", r * (GB // 2) + turn + 1)
                send(r, q, turn)

            turns = TILES0 // RING
            pool.wait_ge(sem("fill_out1"), 16 * 4)
            pool.wait_ge(sem("slots_ready"), 2)
            g.memset(toep[0].rearrange("p a b c -> p (a b c)"), 0.0).then_inc(sem("toep_zero"), 1)
            with pool.Fori(0, 2 * GB // RING) as turn:
                for q in range(RING):
                    piece_out(1, RING // 4 * turn + q // 4, q % 4)
                    result_out(turn, q)
            for visit in range(2 * GB // RING, turns):
                for q in range(RING):
                    result_out(visit, q)
            with pool.Fori(turns, 2 * turns) as visit:
                for q in range(RING):
                    result_out(visit, q)

            pool.wait_ge(sem("y_ready"), GROUPS * TILES0)
            g.memset(toep[1].rearrange("p a b c -> p (a b c)"), 0.0).then_inc(sem("toep_zero"), 1)

            pool.wait_ge(sem("convb_in"), 16)
            with pool.Fori(0, NBLK // 4) as n:
                alone("xn3_ready", n + 1)
                part = xt[:, bass.ds(4 * n, 4), :]
                g.tensor_tensor(part, part, conv_b.rearrange("p (a c) -> p a c", a=1).to_broadcast([P, 4, P]), ALU.add
                                ).then_inc(sem("biased"), 1)

            pool.wait_ge(sem("fill_out2"), 16 * (TILES0 // RING - 1))
            for r in (2, 3):
                with pool.Fori(0, GB // 2) as turn:
                    for q in range(4):
                        piece_out(r, turn, q)
            per = CT // QT
            with pool.Fori(0, E8 // 2) as pair:
                for n in range(2 * per):
                    m, u = n % per, n % 2
                    alone("yq_ready", 2 * per * pair + n + 1)
                    for q in range(QT):
                        g.indirect_dma_start(results, bass.IndirectOffsetOnAxis(ap=quad_in[m][:, q, P:P + 1].bitcast(U32), axis=0),
                                             y_quad[u][:, q, :], None, bounds_check=2 * TOKENS - 1, oob_is_err=False
                                             ).then_inc(sem(f"yq_out{m}"), 16)

        @block.tensor
        def _(pe):
            t = nc.tensor
            pe.wait_ge(sem("pool_const"), 1)
            pe.wait_ge(sem("const_in"), 16 * 7)
            t.transpose(gp[0][:, 0:P], dw_s[:, 0:P], ident)
            t.transpose(gp[0][:, P:2 * P], dw_s[:, P:2 * P], ident).then_inc(sem("wt_done"), 1)
            pe.wait_ge(sem("w1t_ready"), 1)
            pe.wait_ge(sem("gus_in"), 16)
            for j in range(8):
                dst = tp[j % 2]
                if j >= 2:
                    pe.wait_ge(sem("wg_ready"), j - 1)
                for k in range(KB):
                    m = t.matmul(dst[:, P * k:P * k + P], gus_s[:, j, P * k:P * k + P], w1t, start=True, stop=True)
                m.then_inc(sem("wg_done"), 1)
            pe.wait_ge(sem("wg_ready"), 8)

            def visit(i, s, front, mid, back):
                c = 1 - s

                def product(j):
                    if not mid:
                        return
                    if not (isinstance(i, int) and i == 1 and j < 2):
                        pe.wait_ge(sem("z_ready"), 8 * (i - 1) + j - 1)
                    dst = zp[j % 2][:, 0:2 * P].rearrange("p (b c) -> p b c", b=2)
                    for k in range(KB):
                        t.matmul(dst, wg[:, j, k, :], xs[c][:, :, k, 0:P], start=(k == 0), stop=False)
                    if j == 0:
                        pe.wait_ge(sem("g2r_in"), 256 * i)
                    t.matmul(dst, w2t, g2r[c][:, :, j, :], start=False, stop=True).then_inc(sem("z_done"), 1)

                product(0)
                product(1)
                if isinstance(i, int) and i == 6:
                    ranks(0)
                if front:
                    pe.wait_ge(sem("x_in"), 16 * (i + 1))
                    if not (isinstance(i, int) and i == 0):
                        pe.wait_ge(sem("exp_ready"), 8 * i)
                    for b in range(2):
                        for k in range(KB):
                            m = t.transpose(tp[b][:, P * k:P * k + P], xc[:, b, P * k:P * k + P], ident)
                        m.then_inc(sem("f1_done"), 1)
                if back:
                    for b in range(2):
                        pe.wait_ge(sem("x1_ready"), 2 * (i - 2) + b + 1)
                        if front:
                            pe.wait_ge(sem("xs_out"), 2 * i + b + 1)
                        elif isinstance(i, int):
                            pe.wait_ge(sem("exp_ready"), 8 * PAIRS)
                            if i > PAIRS:
                                pe.wait_ge(sem("tnc_ready"), 2 * (PAIRS - 1))
                        for k in range(KB):
                            m = t.transpose(tp[b][:, P * k:P * k + P], zz[s][:, b, P * k:P * k + P], ident)
                        m.then_inc(sem("d1_done"), 1)
                        if b == 0:
                            product(2)
                else:
                    product(2)
                product(3)
                if front:
                    for b in range(2):
                        pe.wait_ge(sem("xn_ready"), 2 * i + b + 1)
                        if back:
                            pe.wait_ge(sem("xt_ready"), 2 * (i - 2) + b + 1)
                        else:
                            pe.wait_ge(sem("xs_out"), 2 * i + b + 1)
                        for k in range(KB):
                            m = t.transpose(tp[b][:, P * k:P * k + P], xs[s][:, b, k, 0:P], ident)
                        m.then_inc(sem("f2_done"), 1)
                product(4)
                if front:
                    pe.wait_ge(sem("xnc_ready"), 2 * i + 2)
                    if not (isinstance(i, int) and i == 0):
                        pe.wait_ge(sem("g2_ready"), 8 * i)
                    if isinstance(i, int) and i == 6:
                        pe.wait_ge(sem("ranks_read"), 1)
                    t.matmul(gp[0][0:hid, 0:2], w1t_se, xsum, start=True, stop=True).then_inc(sem("se1_done"), 1)
                if back:
                    for b in range(2):
                        pe.wait_ge(sem("tn_ready"), 2 * (i - 2) + b + 1)
                        if not front:
                            pe.wait_ge(sem("xt_ready"), 2 * (i - 2) + b + 1)
                        for k in range(KB):
                            m = t.transpose(tp[b][:, P * k:P * k + P], tn[:, k, :], ident)
                        m.then_inc(sem("d3_done"), 1)
                product(5)
                if front:
                    pe.wait_ge(sem("hid_ready"), i + 1)
                    t.matmul(gp[0][:, 8:10], w2t_se[0:hid, :], hidden[0:hid, :], start=True, stop=True
                             ).then_inc(sem("se2_done"), 1)
                if back:
                    for b in range(2):
                        pe.wait_ge(sem("tnc_ready"), 2 * (i - 2) + b + 1)
                        if b == 0 and isinstance(i, int) and i > PAIRS:
                            pe.wait_ge(sem("lg_ready"), i - 2)
                        if not front:
                            pe.wait_ge(sem("g2_ready"), 8 * PAIRS)
                        for k in range(KB):
                            m = t.matmul(gp[1][:, 256 + E8 * (KB * b + k):256 + E8 * (KB * b + k + 1)], tnc[:, k, :],
                                         moe_wg_s, start=True, stop=True)
                        m.then_inc(sem("lg_done"), 1)
                if front:
                    pe.wait_ge(sem("gate_ready"), i + 1)
                    if back:
                        pe.wait_ge(sem("lg_ready"), i - 1)
                    for b in range(2):
                        m = t.matmul(gp[1][:, P * b:P * b + P], gatey[:, b:b + 1].to_broadcast([P, P]), ident,
                                     start=True, stop=True)
                    m.then_inc(sem("gb_done"), 1)
                    if back:
                        pe.wait_ge(sem("tnc_ready"), 2 * (i - 2) + 2)
                    for b in range(2):
                        pe.wait_ge(sem("sig_ready"), 2 * i + b + 1)
                        if b == 1:
                            pe.wait_ge(sem("exp_ready"), 8 * i + 4)
                        for k in range(KB):
                            m = t.matmul(tp[k // 4][:, 256 * (k % 4):256 * (k % 4) + WIN],
                                         sig[:, b, IMG + P * k:IMG + P * k + P], sig[:, b, P * k:P * k + WIN],
                                         start=True, stop=True)
                            if k % 2:
                                m.then_inc(sem("gram_done"), 1)
                        product(6 + b)
                        if b == 0:
                            pe.wait_ge(sem("xs_ready"), i + 1)
                        for kk in range(4):
                            pe.wait_ge(sem("ee_ready"), 4 * (2 * i + b) + min(4, kk + 2))
                            if b or kk >= 2:
                                pe.wait_ge(sem("g2_ready"), 4 * (2 * i + b) + kk - 1)
                            for k in (2 * kk, 2 * kk + 1):
                                dst = gp[kk % 2][:, 256 * (k % 2):256 * (k % 2) + P + 1]
                                rhs = xs[s][:, b, k, 0:P + 1]
                                m = t.matmul(dst, ee[:, k, IMG:IMG + P], rhs, start=True, stop=True)
                                if k:
                                    m = t.matmul(dst[0:IMG], ee[96:P, k - 1, IMG + P:WIN], xs[s][96:P, b, k - 1, 0:P + 1],
                                                 start=False, stop=True, skip_group_check=True, tile_position=(96, 0))
                                if k < KB - 1:
                                    m = t.matmul(dst[96:P], ee[0:IMG, k + 1, 0:IMG], xs[s][0:IMG, b, k + 1, 0:P + 1],
                                                 start=False, stop=True, skip_group_check=True, tile_position=(0, 96))
                            m.then_inc(sem("at_done"), 1)
                else:
                    product(6)
                    product(7)

            def ranks(r):
                pe.wait_ge(sem("picked"), r + 1)
                if r < 2:
                    pe.wait_ge(sem("g2_ready"), (48, 64)[r])
                    pe.wait_ge(sem("lg_ready"), (4, 8)[r])
                else:
                    pe.wait_ge(sem("ranks_read"), r)
                mask_r = e_tmp[:, 2].rearrange("p k e -> p (k e)")
                t.matmul(gp[0][:, :], upper, mask_r, start=True, stop=True)
                t.matmul(gp[1][:, :], ones, mask_r, start=True, stop=True).then_inc(sem("ranked"), 1)

            pipeline(pe, visit)
            ranks(1)

            turns = TILES0 // RING
            pe.wait_ge(sem("moe_in"), 64)
            pe.wait_ge(sem("ranks_read"), 2)

            def expert_tiles(g):
                te = tile_expert[g].bitcast(I32)

                def up(turn, q, first=False):
                    T = g * TILES0 + RING * turn + q
                    pe.wait_ge(sem(f"tile_in{q}"), 16 * (g * turns + turn + 1))
                    if not (g == 0 and first):
                        pe.wait_ge(sem("tok_t_ready"), T)
                    t.transpose(gp[0][:, 0:P], tile_in[q][:, 0:P], ident).then_inc(sem("tok_t_done"), 1)

                def down_1(T, u):
                    pe.wait_ge(sem("act_ready"), T + 1)
                    for c in range(FC0):
                        m = t.transpose(zp[u][:, P * c:P * c + P], act_h[u][:, P * c:P * c + P], ident)
                    m.then_inc(sem("act_t_done"), 1)

                def down_2(n, u, e):
                    T = g * TILES0 + n
                    pe.wait_ge(sem("act_t_ready"), T + 1)
                    if not (g == 0 and isinstance(n, int) and n == 0):
                        pe.wait_ge(sem("y_ready"), T)
                    for c in range(FC0):
                        m = t.matmul(gp[1][:, 0:P], act_t[u][:, c, :], m2_s[:, bass.ds(e, 1), c, :], start=(c == 0),
                                     stop=(c == FC0 - 1))
                    m.then_inc(sem("y_done"), 1)

                def expert(n):
                    return pe.value_load(te[0:1, bass.ds(n, 1)], min_val=0, max_val=E8 - 1)

                def stretch(turn, first, last):
                    e_old = None if first else expert(RING * turn - 1)
                    e = expert(RING * turn)
                    for j in range(RING):
                        n, u = RING * turn + j, j % 2
                        T = g * TILES0 + n
                        pe.wait_ge(sem("tok_t_ready"), T + 1)
                        t.matmul(tp[0][:, 512 * u:512 * u + F0], tok_t[u], m1_s[:, bass.ds(e * F0, F0)], start=True, stop=True
                                 ).then_inc(sem("h_done"), 1)
                        e_next = expert(n + 1) if j < RING - 1 else None
                        old = not (first and j == 0)
                        if old:
                            down_1(T - 1, 1 - u)
                        if not (last and j == RING - 1):
                            up(turn + (j + 1) // RING, (j + 1) % RING)
                        t.matmul(tp[1][:, 512 * u:512 * u + F0], tok_t[u], m3_s[:, bass.ds(e * F0, F0)], start=True, stop=True
                                 ).then_inc(sem("g_done"), 1)
                        if old:
                            down_2(n - 1, 1 - u, e_old)
                        e_old, e = e, e_next
                    if last:
                        down_1(T, u)
                        down_2(n, u, e_old)

                up(0, 0, first=True)
                stretch(0, True, False)
                with pe.Fori(1, turns - 1) as turn:
                    stretch(turn, False, False)
                stretch(turns - 1, False, True)

            for g in range(GROUPS):
                pe.wait_ge(sem("slots_ready"), g + 1)
                expert_tiles(g)

            pe.wait_ge(sem("xn3_ready"), NBLK // 4)
            pe.wait_ge(sem("y_ready"), GROUPS * TILES0)

            def channels(turn):
                for n in range(8):
                    s, cc = (n // 2) % 2, 4 * (n % 2)
                    if n % 2 == 0:
                        pe.wait_ge(sem(f"toep_in{s}"), 64 * (2 * turn + n // 4 + 1))
                    if not isinstance(turn, int):
                        pe.wait_ge(sem("x3_ready"), 8 * turn)
                    for c in range(4):
                        chan = 32 * turn + 4 * n + c
                        dst = banks[n][:, P * c:P * c + P]
                        src = xn[:, :, bass.ds(chan, 1)].rearrange("p k c -> p (k c)")
                        w = toep[s].rearrange("p a x c -> p (a x) c")
                        t.matmul(dst, w[:, P:2 * P, cc + c], src, start=True, stop=True)
                        dk, sk = (z.rearrange("p (b k) -> p b k", b=B) for z in (dst, src))
                        t.matmul(dk[:, :, 0:KB - 1], w[:, 0:P, cc + c], sk[:, :, 1:KB], start=False, stop=True,
                                 skip_group_check=True)
                        m = t.matmul(dk[:, :, 1:KB], w[:, 2 * P:3 * P, cc + c], sk[:, :, 0:KB - 1], start=False, stop=True,
                                     skip_group_check=True)
                    m.then_inc(sem("conv_done"), 1)

            repeat(pe, 0, NCG // 4, channels)

            pe.wait_ge(sem("x3_ready"), C // 4)

            def router(turn):
                for u in range(2):
                    n = 2 * turn + u
                    pe.wait_ge(sem("tn4_ready"), n + 1)
                    if not isinstance(turn, int):
                        pe.wait_ge(sem("tnc4_ready"), 2 * turn)
                    for k in range(KB):
                        m = t.transpose(tp[u][:, P * k:P * k + P], tn4[u][:, k, :], ident)
                    m.then_inc(sem("tn4_done"), 1)
                    pe.wait_ge(sem("tnc4_ready"), n + 1)
                    if not isinstance(turn, int):
                        pe.wait_ge(sem("lg4_ready"), 2 * turn)
                    for k in range(KB):
                        m = t.matmul(zp[u][:, E8 * k:E8 * k + E8], tnc4[u][:, k, :], gate_s, start=True, stop=True)
                    m.then_inc(sem("lg4_done"), 1)

            repeat(pe, 0, NBLK // KB // 2, router)
            ranks(2)
            ranks(3)

            per = CT // QT

            def quad_up(pair, n, first=False):
                Q, m = 2 * per * pair + n, n % per
                pe.wait_ge(sem(f"quad_in{m}"), 16 * (2 * pair + n // per + 1))
                if not first:
                    pe.wait_ge(sem("quad_t_ready"), Q)
                for q in range(QT):
                    last = t.transpose(gp[0][:, P * q:P * q + P], quad_in[m][:, q, 0:P], ident)
                last.then_inc(sem("quad_t_done"), 1)

            def quad_down(Q, u, s):
                pe.wait_ge(sem("hid_t_ready"), 4 * Q + 4)
                for q in range(QT):
                    for c in range(FC1):
                        m = t.matmul(zp[u][:, P * q:P * q + P], hid_t[u][:, c, P * q:P * q + P], fw2[s][:, c, :],
                                     start=(c == 0), stop=(c == FC1 - 1))
                m.then_inc(sem("yq_done"), 1)

            def expert_pair(pair, first, last):
                for n in range(2 * per):
                    Q, u, s = 2 * per * pair + n, n % 2, n // per
                    if n % per == 0:
                        pe.wait_ge(sem(f"expert_in{s}"), 64 * (pair + 1))
                    pe.wait_ge(sem("quad_t_ready"), Q + 1)
                    for c in range(FC1):
                        if not (first and n == 0):
                            pe.wait_ge(sem("hid_t_ready"), 4 * (Q - 1) + c + 1)
                        t.matmul(tp[c // 2][:, 512 * (c % 2):512 * (c % 2) + 512], fw1[s][:, P * c:P * c + P], quad_t[u],
                                 start=True, stop=True).then_inc(sem("hq_done"), 1)
                        if c == 1 and not (last and n == 2 * per - 1):
                            quad_up(pair if n < 2 * per - 1 else pair + 1, (n + 1) % (2 * per))
                    if not (first and n == 0):
                        if not (first and n < 3):
                            pe.wait_ge(sem("yq_ready"), Q - 2)
                        quad_down(Q - 1, 1 - u, ((n - 1) // per) % 2)
                if last:
                    pe.wait_ge(sem("yq_ready"), Q - 1)
                    quad_down(Q, u, s)

            pe.wait_ge(sem("ranks_read"), 4)
            quad_up(0, 0, first=True)
            expert_pair(0, True, False)
            with pe.Fori(1, E8 // 2 - 1) as pair:
                expert_pair(pair, False, False)
            expert_pair(E8 // 2 - 1, False, True)

            pe.wait_ge(sem("yq_ready"), E8 * CT // QT)

            def output(turn):
                for u in range(2):
                    pe.wait_ge(sem("fin_ready"), 2 * turn + u + 1)
                    if not isinstance(turn, int):
                        pe.wait_ge(sem("fin_t_ready"), 2 * turn)
                    for k in range(KB // 2):
                        m = t.transpose(tp[u][:, P * k:P * k + P], fin[u][:, k, :], ident)
                    m.then_inc(sem("fin_t_done"), 1)

            repeat(pe, 0, NBLK // 8, output)

        @block.scalar
        def _(act):
            A = nc.scalar.activation

            def visit(i, s, front, mid, back):
                def z_out(j):
                    if mid:
                        act.wait_ge(sem("z_done"), 8 * (i - 1) + j + 1)
                        A(zz[1 - s][:, :, P * j:P * j + P], zp[j % 2][:, 0:2 * P].rearrange("p (b c) -> p b c", b=2),
                          ACT.Copy).then_inc(sem("z_ready"), 1)

                if back:
                    for b in range(2):
                        act.wait_ge(sem("zsc_ready"), i - 1)
                        A(zz[s][:, b, :], zz[s][:, b, :], ACT.Identity, bias=znm[:, b:b + 1], scale=zsc[:, b:b + 1]
                          ).then_inc(sem("zn_ready"), 1)
                if front:
                    for b in range(2):
                        act.wait_ge(sem("f1_done"), 2 * i + b + 1)
                        if b == 0 and not (isinstance(i, int) and i < 2):
                            act.wait_ge(sem("z_done"), 8 * (i - 1))
                        A(xs[s][:, b, :, 0:P], tp[b][:, :].rearrange("p (k c) -> p k c", k=KB), ACT.Copy
                          ).then_inc(sem("xs_out"), 1)
                z_out(0)
                z_out(1)
                if back:
                    for b in range(2):
                        act.wait_ge(sem("d1_done"), 2 * (i - 2) + b + 1)
                        A(xt[:, bass.ds(2 * KB * (i - 2) + KB * b, KB), :], tp[b][:, :].rearrange("p (k c) -> p k c", k=KB),
                          ACT.Copy).then_inc(sem("xt_ready"), 1)
                        z_out(2 + b)
                else:
                    z_out(2)
                    z_out(3)
                if front:
                    for b in range(2):
                        act.wait_ge(sem("f2_done"), 2 * i + b + 1)
                        if not (isinstance(i, int) and i == 0):
                            act.wait_ge(sem("gram_done"), 8 * i)
                        A(sig[:, b, IMG:IMG + HW], tp[b][:, :], ACT.Copy, accum_out=xsum[:, b:b + 1]
                          ).then_inc(sem("xnc_ready"), 1)
                z_out(4)
                if front:
                    act.wait_ge(sem("se1_done"), i + 1)
                    A(hidden[0:hid, :], gp[0][0:hid, 0:2], ACT.Relu, bias=b1_se[0:hid, :], scale=1.0 / HW
                      ).then_inc(sem("hid_ready"), 1)
                if back:
                    for b in range(2):
                        act.wait_ge(sem("d3_done"), 2 * (i - 2) + b + 1)
                        if b:
                            act.wait_ge(sem("lg_done"), 2 * (i - 2) + b)
                        elif isinstance(i, int) and i > PAIRS:
                            act.wait_ge(sem("lg_done"), 2 * (i - 2))
                        A(tnc, tp[b][:, :].rearrange("p (k c) -> p k c", k=KB), ACT.Copy).then_inc(sem("tnc_ready"), 1)
                        if b == 0:
                            z_out(5)
                else:
                    z_out(5)
                if front:
                    act.wait_ge(sem("se2_done"), i + 1)
                    A(gatey, gp[0][:, 8:10], ACT.Sigmoid, bias=b2_se).then_inc(sem("gate_ready"), 1)
                    for b in range(2):
                        if b == 0:
                            act.wait_ge(sem("gate_ready"), i + 1)
                        A(sig[:, b, IMG:IMG + HW], sig[:, b, IMG:IMG + HW], ACT.Sigmoid, scale=gatey[:, b:b + 1]
                          ).then_inc(sem("sig_ready"), 1)
                    for b in range(2):
                        for kk in range(4):
                            act.wait_ge(sem("gram_done"), 4 * (2 * i + b) + kk + 1)
                            if kk == 0 and b:
                                act.wait_ge(sem("at_done"), 8 * i + 4)
                            elif kk == 0 and not (isinstance(i, int) and i == 0):
                                act.wait_ge(sem("at_done"), 8 * i)
                            src = tp[kk // 2][:, 512 * (kk % 2):512 * (kk % 2) + 512].rearrange("p (a w) -> p a w", a=2)
                            A(ee[:, 2 * kk:2 * kk + 2, :], src[:, :, 0:WIN], ACT.Exp, scale=1.0 / C
                              ).then_inc(sem("exp_ready"), 1)
                        z_out(6 + b)
                else:
                    z_out(6)
                    z_out(7)

            def weights(r):
                act.wait_ge(sem("gap"), r + 1)
                part = slice(GB * (r % 2), GB * (r % 2) + GB)
                A(weight[:, 0, part], top[:, 2, :], ACT.Sigmoid)
                A(weight[:, 1, part], top[:, 2, :], ACT.Sigmoid, scale=-1.0).then_inc(sem("weighed"), 1)

            pipeline(act, visit, weights)

            turns = TILES0 // RING

            def hidden_out(T, u):
                act.wait_ge(sem("h_done"), T + 1)
                A(act_h[u], tp[0][:, 512 * u:512 * u + F0], ACT.Silu).then_inc(sem("silu_ready"), 1)

            def act_t_out(T, u):
                act.wait_ge(sem("act_t_done"), T + 1)
                A(act_t[u].rearrange("p a b -> p (a b)"), zp[u][:, 0:F0], ACT.Copy).then_inc(sem("act_t_ready"), 1)

            def tok_t_out(T, u):
                act.wait_ge(sem("tok_t_done"), T + 1)
                A(tok_t[u], gp[0][:, 0:P], ACT.Copy).then_inc(sem("tok_t_ready"), 1)

            def turn_tiles(g, turn, first, last, beside=None):
                for q in range(RING):
                    T, u = g * TILES0 + RING * turn + q, q % 2
                    if not (first and q == 0):
                        act_t_out(T - 1, 1 - u)
                    hidden_out(T, u)
                    if not (last and q == RING - 1):
                        tok_t_out(T + 1, 1 - u)
                    if beside is not None and q < KB // 2:
                        normalise(*beside, q)
                if last:
                    act_t_out(T, u)

            def normalise(n, u, k):
                if k == 0:
                    act.wait_ge(sem("stats3"), n + 1)
                flat = lambda z: z.rearrange("p a c -> p (a c)")
                blk = KB // 2 * n + k
                done = A(flat(xn[:, bass.ds(blk, 1), :]), flat(xt[:, bass.ds(blk, 1), :]), ACT.Identity,
                         bias=mean_c[u][:, k:k + 1], scale=rstd_c[u][:, k:k + 1])
                if k == KB // 2 - 1:
                    done.then_inc(sem("xn3_ready"), 1)

            tok_t_out(0, 0)
            turn_tiles(0, 0, True, False)
            with act.Fori(1, turns - 1) as turn:
                turn_tiles(0, turn, False, False)
            turn_tiles(0, turns - 1, False, True)
            tok_t_out(TILES0, 0)
            turn_tiles(1, 0, True, False)
            turn_tiles(1, 1, False, False, beside=(0, 0))
            with act.Fori(1, turns // 2) as turn:
                for v in range(2):
                    turn_tiles(1, 2 * turn + v, False, False, beside=(2 * turn + v - 1, 1 - v))
            turn_tiles(1, turns - 1, False, True, beside=(turns - 2, 1))

            with act.Fori(NBLK // 16, NBLK // 8) as turn:
                for u in range(2):
                    for k in range(KB // 2):
                        normalise(2 * turn + u, u, k)

            def router(turn):
                for u in range(2):
                    act.wait_ge(sem("tn4_done"), 2 * turn + u + 1)
                    if not isinstance(turn, int):
                        act.wait_ge(sem("lg4_done"), 2 * turn)
                    A(tnc4[u].rearrange("p a b -> p (a b)"), tp[u][:, :], ACT.Copy).then_inc(sem("tnc4_ready"), 1)

            repeat(act, 0, NBLK // KB // 2, router)
            weights(2)
            weights(3)

            per = CT // QT

            def quad_t_out(Q, u):
                act.wait_ge(sem("quad_t_done"), Q + 1)
                A(quad_t[u], gp[0][:, :], ACT.Copy).then_inc(sem("quad_t_ready"), 1)

            def gelu_pair(pair, last):
                for n in range(2 * per):
                    Q, u, s = 2 * per * pair + n, n % 2, n // per
                    for c in range(FC1):
                        act.wait_ge(sem("hq_done"), 4 * Q + c + 1)
                        A(hid_t[u][:, c, :], tp[c // 2][:, 512 * (c % 2):512 * (c % 2) + 512], ACT.Gelu,
                          bias=fb1[s][:, c:c + 1]).then_inc(sem("hid_t_ready"), 1)
                        if c == 1 and not (last and n == 2 * per - 1):
                            quad_t_out(Q + 1, 1 - u)

            quad_t_out(0, 0)
            with act.Fori(0, E8 // 2 - 1) as pair:
                gelu_pair(pair, False)
            gelu_pair(E8 // 2 - 1, True)

            def output(turn):
                for u in range(2):
                    n = 2 * turn + u
                    act.wait_ge(sem("fin_t_done"), n + 1)
                    if not isinstance(turn, int):
                        act.wait_ge(sem(f"out_done{u}"), 16 * turn)
                    A(fin_t[u], tp[u][:, 0:512], ACT.Copy).then_inc(sem("fin_t_ready"), 1)
                    act.wait_ge(sem("fin_t_ready"), n + 1)
                    act.dma_start(out[bass.ds(turn, 1), :, 512 * u:512 * u + 512].rearrange("b c p -> c (b p)"), fin_t[u]
                                  ).then_inc(sem(f"out_done{u}"), 16)

            repeat(act, 0, NBLK // 8, output)
            for u in range(2):
                act.wait_ge(sem(f"out_done{u}"), 16 * (NBLK // 8))

        @block.vector
        def _(dve):
            v = nc.vector
            cst = Order(dve, sem("dve_const"), 0, 10)
            dve.wait_ge(sem("iotas"), 1)
            v.tensor_scalar(code_idx.bitcast(I32), code_idx.bitcast(I32), CODES - 1, None, ALU.bitwise_and
                            ).then_inc(sem("code_idx"), 1)
            dve.wait_ge(sem("pool_const"), 1)
            ti = t32[:, 0:1].bitcast(I32)
            cst.link(v.tensor_scalar(ti, ti, IMG - 1, None, ALU.bitwise_and))
            cst.link(v.tensor_copy(t32[:, 1:2], ti))
            cst.link(v.tensor_scalar(t32[:, 2:3], t32[:, 1:2], 0.0, None, ALU.is_equal))
            cst.link(v.tensor_scalar(t32[:, 3:4], t32[:, 1:2], float(IMG - 1), None, ALU.is_equal))
            cst.link(v.tensor_tensor(t32[:, 2:3], t32[:, 2:3], t32[:, 3:4], ALU.add))
            cst.link(v.tensor_scalar(t32[:, 2:3], t32[:, 2:3], -1.0, 3.0, ALU.mult, ALU.add))
            cst.link(v.tensor_scalar(npad, npad, t32[:, 2:3], None, ALU.mult))
            cst.link(v.tensor_scalar(npad, npad, -1.0, 9.0, ALU.mult, ALU.add))
            dve.wait_ge(sem("wt_done"), 1)
            cst.link(v.tensor_copy(w2t, gp[0][:, P:2 * P]))
            v.tensor_copy(w1t, gp[0][:, 0:P]).then_inc(sem("w1t_ready"), 1)
            cst.step(v.memset(t32[:, 5:6], 0.0))
            cst.end()
            for j in range(8):
                dve.wait_ge(sem("wg_done"), j + 1)
                v.tensor_copy(wg[:, j].rearrange("p k c -> p (k c)"), tp[j % 2][:, :]).then_inc(sem("wg_ready"), 1)

            def visit(i, s, front, mid, back):
                if back:
                    o = Order(dve, sem("dve_zstat"), i - 2, 16)
                    dve.wait_ge(sem("z_ready"), 8 * (i - 1))
                    for b in range(2):
                        for h in range(2):
                            o.step(v.bn_stats(zst[:, 2 * b + h, :], zz[s][:, b, 512 * h:512 * h + 512]))
                    o.settle()
                    o.step(v.memset(t32[:, 5:6], 0.0))
                    for b in range(2):
                        last = v.bn_aggr(zmv[:, b, :], zst[:, 2 * b:2 * b + 2, :])
                    o.link(last)
                    v.tensor_scalar(ln_var[:, 0:2], zmv[:, :, 1], 1e-5, None, ALU.add).then_inc(sem("zvar"), 1)
                    dve.wait_ge(sem("zvar"), i - 1)
                    last = rsqrt(v, o, ln_var[:, 0:2], rs_int[:, 0:2].bitcast(I32), rs_tmp[:, 0:2],
                                 lambda t, y: v.scalar_tensor_tensor(out=zsc, in0=t, scalar=1.5, in1=y,
                                                                     op0=ALU.add, op1=ALU.mult))
                    last.then_inc(sem("zsc_own"), 1)
                    dve.wait_ge(sem("zsc_own"), i - 1)
                    v.scalar_tensor_tensor(out=znm, in0=zmv[:, :, 0], scalar=-1.0, in1=zsc, op0=ALU.mult, op1=ALU.mult
                                           ).then_inc(sem("zsc_ready"), 1)
                    o.end()
                    for b in range(2):
                        dve.wait_ge(sem("zn_ready"), 2 * (i - 2) + b + 1)
                        v.scalar_tensor_tensor(out=zz[s][:, b, :], in0=zz[s][:, b, :], scalar=0.2, in1=zz[s][:, b, :],
                                               op0=ALU.mult, op1=ALU.max).then_inc(sem("leaky"), 1)
                        dve.wait_ge(sem("leaky"), 2 * (i - 2) + b + 1)
                        dve.wait_ge(sem("res_in"), 16 * (2 * (i - 2) + b + 1))
                        v.tensor_tensor(zz[s][:, b, :], zz[s][:, b, :], xr, ALU.add).then_inc(sem("x1_ready"), 1)
                if front:
                    for b in range(2):
                        dve.wait_ge(sem("xs_out"), 2 * i + b + 1)
                        for k in range(KB):
                            last = v.bn_stats(st[:, KB * b + k, :], xs[s][:, b, k, 0:P])
                    o = Order(dve, sem("dve_front"), i, 18)
                    o.link(last)
                    token_stats(v, o, st, mean_f, ln_var, rs_tmp, 1e-6, 2 * KB)
                    last = rsqrt(v, o, ln_var, rs_int.bitcast(I32), rs_tmp,
                                 lambda t, y: v.scalar_tensor_tensor(out=rstd_f, in0=t, scalar=1.5, in1=y,
                                                                     op0=ALU.add, op1=ALU.mult))
                    last.then_inc(sem("rstd_f"), 1)
                    dve.wait_ge(sem("rstd_f"), i + 1)
                    for b in range(2):
                        for k in range(KB):
                            w = xs[s][:, b, k, 0:P]
                            last = v.tensor_scalar(w, w, mean_f[:, KB * b + k:KB * b + k + 1], rstd_f[:, KB * b + k:KB * b + k + 1],
                                                   ALU.subtract, ALU.mult)
                        last.then_inc(sem("xn_ready"), 1)
                    o.end()
                if back:
                    for b in range(2):
                        o = Order(dve, sem("dve_back"), 2 * (i - 2) + b, 18)
                        blk = 2 * KB * (i - 2) + KB * b
                        dve.wait_ge(sem("xt_ready"), 2 * (i - 2) + b + 1)
                        for k in range(KB):
                            last = v.bn_stats(st[:, k, :], xt[:, bass.ds(blk + k, 1), :])
                        o.link(last)
                        token_stats(v, o, st, ln_mean[:, bass.ds(blk, KB)], ln_var[:, 0:KB], rs_tmp[:, 0:KB], 1e-5, KB)
                        last = rsqrt(v, o, ln_var[:, 0:KB], rs_int[:, 0:KB].bitcast(I32), rs_tmp[:, 0:KB],
                                     lambda t, y: v.scalar_tensor_tensor(out=ln_rstd[:, bass.ds(blk, KB)], in0=t,
                                                                         scalar=1.5, in1=y, op0=ALU.add, op1=ALU.mult))
                        last.then_inc(sem("rstd_b"), 1)
                        dve.wait_ge(sem("rstd_b"), 2 * (i - 2) + b + 1)
                        if b:
                            dve.wait_ge(sem("d3_done"), 2 * (i - 2) + b)
                        for k in range(KB):
                            last = v.tensor_scalar(tn[:, k, :], xt[:, bass.ds(blk + k, 1), :].rearrange("p a c -> p (a c)"),
                                                   ln_mean[:, bass.ds(blk + k, 1)], ln_rstd[:, bass.ds(blk + k, 1)],
                                                   ALU.subtract, ALU.mult)
                        last.then_inc(sem("tn_ready"), 1)
                        o.end()
                    dve.wait_ge(sem("lg_done"), 2 * (i - 2) + 2)
                    v.tensor_copy(logits[:, bass.ds(2 * KB * (i - 2), 2 * KB), :],
                                  gp[1][:, 256:256 + 2 * KB * E8].rearrange("p (k e) -> p k e", e=E8)
                                  ).then_inc(sem("lg_ready"), 1)
                if front:
                    dve.wait_ge(sem("gb_done"), i + 1)
                    dve.wait_ge(sem("f2_done"), 2 * i + 2)
                    for b in range(2):
                        gb = gp[1][:, P * b:P * b + P].rearrange("p (a c) -> p a c", a=1).to_broadcast([P, KB, P])
                        last = v.tensor_tensor(xs[s][:, b, :, 0:P], xs[s][:, b, :, 0:P], gb, ALU.mult)
                    last.then_inc(sem("xs_ready"), 1)
                    for b in range(2):
                        for kk in range(4):
                            dve.wait_ge(sem("exp_ready"), 4 * (2 * i + b) + kk + 1)
                            mk = mask.rearrange("p a b -> p (a b)").rearrange("p (a w) -> p a w", a=1).to_broadcast([P, 2, WIN])
                            v.tensor_tensor(ee[:, 2 * kk:2 * kk + 2, :], ee[:, 2 * kk:2 * kk + 2, :], mk, ALU.mult
                                            ).then_inc(sem("ee_ready"), 1)
                        if b:
                            dve.wait_ge(sem("g2r_in"), 128 * (2 * i + b))
                        elif not (isinstance(i, int) and i == 0):
                            dve.wait_ge(sem("g2r_in"), 256 * i)
                        o = Order(dve, sem("dve_g2"), 2 * i + b, 8)
                        if b or not (isinstance(i, int) and i == 0):
                            dve.wait_ge(sem("g2_ready"), 4 * (2 * i + b))
                        for kk in range(4):
                            dve.wait_ge(sem("at_done"), 4 * (2 * i + b) + kk + 1)
                            src = gp[kk % 2][:, :].rearrange("p (a w) -> p a w", a=2)
                            rd = rden[:, 2 * kk:2 * kk + 2]
                            o.link(v.tensor_tensor(rd, src[:, :, P], npad[:, 2 * kk:2 * kk + 2], ALU.add))
                            o.link(v.reciprocal(rd, rd))
                            v.tensor_tensor(g2n[:, 2 * kk:2 * kk + 2, :], src[:, :, 0:P],
                                            rd.rearrange("p (a c) -> p a c", c=1).to_broadcast([P, 2, P]), ALU.mult
                                            ).then_inc(sem("g2_ready"), 1)
                        o.end()

            def aside(n):
                if n == 1:
                    o = Order(dve, sem("dve_taps"), 0, 3)
                    ti = tap_sign.bitcast(I32)
                    o.link(v.tensor_scalar(ti, ti, 1, None, ALU.bitwise_and))
                    o.link(v.tensor_copy(tap_sign, ti))
                    o.link(v.tensor_scalar(tap_sign, tap_sign, 2.0, -1.0, ALU.mult, ALU.add))
                    o.end()
                    dve.wait_ge(sem("tapw_in"), 16 * KER * KER)
                    v.tensor_tensor(tap_w, tap_w, tap_sign, ALU.mult).then_inc(sem("tapw_ready"), 1)

            route_links = [0]

            def route(r):
                o = Order(dve, sem("dve_route"), 1, route_links[-1])
                half = slice(GB * (r % 2), GB * (r % 2) + GB)
                wide = lambda z: z.rearrange("p (k e) -> p k e", e=1).to_broadcast([P, GB, E8])
                per_e = lambda z: z.rearrange("p (k e) -> p k e", k=1).to_broadcast([P, GB, E8])
                best, second, gap, pick = (top[:, n, :] for n in range(4))
                work, place, both = (e_tmp[:, n] for n in range(3))
                lg = logits[:, half, :]
                dve.wait_ge(sem("lg_ready" if r < 2 else "lg4_ready"), (4, 8, 8, 16)[r])
                if r:
                    dve.wait_ge(sem("weighed"), r)

                def first_of(value, src, hot):
                    o.link(v.tensor_reduce(value, src, AX_X, ALU.max))
                    o.link(v.tensor_tensor(work, src, wide(value), ALU.is_equal))
                    o.link(v.tensor_tensor(work, work, per_e(prefer), ALU.mult))
                    o.link(v.tensor_reduce(pick, work, AX_X, ALU.max))
                    o.link(v.tensor_tensor(hot, work, wide(pick), ALU.is_equal))

                first_of(best, lg, e_hot[:, 0])
                o.link(v.scalar_tensor_tensor(out=both, in0=e_hot[:, 0], scalar=-3.0e38, in1=lg, op0=ALU.mult, op1=ALU.add))
                first_of(second, both, e_hot[:, 1])
                v.tensor_tensor(gap, best, second, ALU.subtract).then_inc(sem("gap"), 1)
                v.tensor_tensor(both, e_hot[:, 0], e_hot[:, 1], ALU.add).then_inc(sem("picked"), 1)

                dve.wait_ge(sem("ranked"), r + 1)
                sums = work.rearrange("p k e -> p (k e)").rearrange("p (e k) -> p e k", e=E8)
                rank, count = (z[:, :].rearrange("p (k e) -> p k e", e=E8) for z in gp)
                for e in range(E8):
                    last = v.tensor_tensor_scan(sums[:, e, :], ones[:, 0:GB], count[:, :, e], 0.0, ALU.mult, ALU.add)
                o.link(last)
                o.link(v.tensor_tensor(place, sums.rearrange("p e k -> p k e"), count, ALU.subtract))
                v.tensor_tensor(place, place, rank, ALU.add).then_inc(sem("ranks_read"), 1)
                dve.wait_ge(sem("ranks_read"), r + 1)
                total = sums[:, :, GB - 1]
                if r < 2:
                    ti = n_tiles.bitcast(I32)
                    o.link(v.tensor_scalar(ti, total, float(P - 1), None, ALU.add))
                    o.link(v.tensor_scalar(ti, ti, P.bit_length() - 1, None, ALU.arith_shift_right))
                    o.link(v.tensor_copy(n_tiles, ti))
                    o.link(v.tensor_tensor_scan(taken, ones[:, 0:E8], n_tiles, 0.0, ALU.mult, ALU.add))
                    o.link(v.tensor_tensor(first_slot, taken, n_tiles, ALU.subtract))
                    o.link(v.tensor_scalar(first_slot, first_slot, float(P), None, ALU.mult))
                    owner = both.rearrange("p k e -> p (k e)")[:, 0:TILES0]
                    o.link(v.tensor_scalar(owner, tile_no, taken[:, 0:1], None, ALU.is_ge))
                    for e in range(1, E8 - 1):
                        o.link(v.scalar_tensor_tensor(out=owner, in0=tile_no, scalar=taken[:, e:e + 1], in1=owner,
                                                      op0=ALU.is_ge, op1=ALU.add))
                    o.link(v.tensor_copy(tile_expert[r].bitcast(I32), owner))
                    o.link(v.tensor_tensor(place, place, per_e(first_slot), ALU.add))
                    for k in range(2):
                        o.link(v.tensor_tensor(both, e_hot[:, k], place, ALU.mult))
                        o.link(v.tensor_reduce(pick, both, AX_X, ALU.add))
                        last = v.tensor_copy(slot[:, k, half].bitcast(I32), pick)
                        if k == 0:
                            o.link(last)
                        else:
                            last.then_inc(sem("slots_ready"), 1)
                else:
                    o.link(v.tensor_tensor(place, place, per_e(carry), ALU.add))
                    o.link(v.tensor_tensor(carry, carry, total, ALU.add))
                    dve.wait_ge(sem("weighed"), r + 1)
                    for k in range(2):
                        o.link(v.tensor_tensor(both, e_hot[:, k], place, ALU.mult))
                        o.link(v.tensor_reduce(pick, both, AX_X, ALU.add))
                        o.link(v.tensor_tensor(both, e_hot[:, k], per_e(cap_base), ALU.mult))
                        o.link(v.tensor_reduce(best, both, AX_X, ALU.add))
                        o.link(v.tensor_tensor(best, best, pick, ALU.add))
                        o.link(v.tensor_scalar(pick, pick, float(CAP), None, ALU.is_ge))
                        o.link(v.scalar_tensor_tensor(out=best, in0=pick, scalar=float(NOWHERE), in1=best,
                                                      op0=ALU.mult, op1=ALU.add))
                        o.link(v.tensor_scalar(pick, pick, -1.0, 1.0, ALU.mult, ALU.add))
                        o.link(v.tensor_tensor(weight[:, k, half], weight[:, k, half], pick, ALU.mult))
                        last = v.tensor_copy(slot[:, k, half].bitcast(I32), best)
                        if k == 0:
                            o.link(last)
                        else:
                            last.then_inc(sem("slots_ready"), 1)
                dve.wait_ge(sem("slots_ready"), r + 1)
                route_links.append(o.base + o.k)

            def make_pieces(r, turn, u):
                blk = GB * (r % 2) + 2 * turn + u
                for k in range(2):
                    q = 2 * u + k
                    dve.wait_ge(sem(f"piece_out{q}"), 16 * (r * (GB // 2) + turn))
                    v.tensor_scalar(piece[:, q, 0:P], xt[:, bass.ds(blk, 1), :].rearrange("p a c -> p (a c)"),
                                    ln_mean[:, bass.ds(blk, 1)], ln_rstd[:, bass.ds(blk, 1)], ALU.subtract, ALU.mult)
                    v.tensor_copy(piece[:, q, P:P + 1].bitcast(I32), row_id[:, k, bass.ds(blk, 1)].bitcast(I32))
                    v.tensor_copy(piece_slot[:, q:q + 1].bitcast(I32), slot[:, k, bass.ds(blk, 1)].bitcast(I32)
                                  ).then_inc(sem(f"piece_made{q}"), 1)

            pipeline(dve, visit, route, aside)

            turns = TILES0 // RING

            def y_out_of(g, turn, q):
                T = g * TILES0 + RING * turn + q
                dve.wait_ge(sem("y_done"), T + 1)
                dve.wait_ge(sem(f"y_out{q}"), 16 * (g * turns + turn))
                v.tensor_copy(y_tile[q], gp[1][:, 0:P]).then_inc(sem("y_ready"), 1)

            def turn_tiles(g, turn, first, last, pieces, beside=None):
                te = tile_expert[g].bitcast(I32)
                for q in range(RING):
                    n, u = RING * turn + q, q % 2
                    T = g * TILES0 + n
                    e = dve.value_load(te[0:1, bass.ds(n, 1)], min_val=0, max_val=E8 - 1)
                    dve.wait_ge(sem("g_done"), T + 1)
                    if not (g == 0 and first and q < 2):
                        dve.wait_ge(sem("act_ready"), T - 1)
                    v.tensor_tensor(act_g[u], tp[1][:, 512 * u:512 * u + F0], b3_s[:, bass.ds(e * F0, F0)], ALU.add
                                    ).then_inc(sem("g_biased"), 1)
                    dve.wait_ge(sem("g_biased"), T + 1)
                    dve.wait_ge(sem("silu_ready"), T + 1)
                    v.tensor_tensor(act_h[u], act_h[u], act_g[u], ALU.mult).then_inc(sem("act_ready"), 1)
                    if not (first and q == 0):
                        y_out_of(g, turn if q else turn - 1, (q - 1) % RING)
                    if pieces and q % 2:
                        make_pieces(1, RING // 4 * turn + q // 4, q // 2 % 2)
                    if beside is not None and 2 <= q < 7:
                        chunk_sum(*beside, q - 2)
                if last:
                    y_out_of(g, turn, q)

            KC = KB // 2
            sums = [None, None]
            flat = lambda z: z.rearrange("p a c -> p (a c)")

            def chunk_sum(n, u, turn, part):
                o = sums[u]
                if part == 0:
                    o = sums[u] = Order(dve, sem("dve_sum"), n, 3 + STAT_LINKS + RSQRT_LINKS)
                    dve.wait_ge(sem(f"y_in{u}"), 16 * (turn + 1))
                if part < 2:
                    if part == 1:
                        o.settle()
                    for k in range(KC):
                        at = flat(xt[:, bass.ds(KC * n + k, 1), :])
                        last = v.scalar_tensor_tensor(out=at, in0=y_in[u][:, k, part, :], scalar=weight[:, part, bass.ds(KC * n + k, 1)],
                                                      in1=at, op0=ALU.mult, op1=ALU.add)
                    if part == 0:
                        o.step(last)
                    else:
                        last.then_inc(sem("x2_ready"), 1)
                elif part == 2:
                    dve.wait_ge(sem("x2_ready"), n + 1)
                    v.memset(idle[:, 0:1], 0.0)
                    for k in range(KC):
                        last = v.bn_stats(st_c[:, k, :], xt[:, bass.ds(KC * n + k, 1), :])
                    o.step(last)
                elif part == 3:
                    o.settle()
                    if not isinstance(n, int):
                        dve.wait_ge(sem("xn3_ready"), n - 1)
                    token_stats(v, o, st_c, mean_c[u], var_c[:, 0:KC], rst_c[:, 0:KC], 1e-6, KC)
                else:
                    last = rsqrt(v, o, var_c[:, 0:KC], rsi_c[:, 0:KC].bitcast(I32), rst_c[:, 0:KC],
                                 lambda t, y: v.scalar_tensor_tensor(out=rstd_c[u], in0=t, scalar=1.5, in1=y,
                                                                     op0=ALU.add, op1=ALU.mult))
                    o.link(last)
                    v.scalar_tensor_tensor(out=mean_c[u], in0=mean_c[u], scalar=-1.0, in1=rstd_c[u], op0=ALU.mult, op1=ALU.mult
                                           ).then_inc(sem("stats3"), 1)
                    o.end()

            turn_tiles(0, 0, True, False, True)
            with dve.Fori(1, 2 * GB // RING) as turn:
                turn_tiles(0, turn, False, False, True)
            for turn in range(2 * GB // RING, turns):
                turn_tiles(0, turn, False, turn == turns - 1, False)
            turn_tiles(1, 0, True, False, False, beside=(0, 0, 0))
            turn_tiles(1, 1, False, False, False, beside=(1, 1, 0))
            with dve.Fori(1, turns // 2) as turn:
                for u in range(2):
                    turn_tiles(1, 2 * turn + u, False, False, False, beside=(2 * turn + u, u, turn))
            turn_tiles(1, turns - 1, False, True, False)

            with dve.Fori(NBLK // 16, NBLK // 8) as turn:
                for u in range(2):
                    for part in range(5):
                        chunk_sum(2 * turn + u, u, turn, part)

            dve.wait_ge(sem("biased"), NBLK // 4)
            with dve.Fori(0, NCG // 4) as turn:
                for n in range(8):
                    at = xt[:, :, bass.ds(32 * turn + 4 * n, 4)]
                    dve.wait_ge(sem("conv_done"), 8 * turn + n + 1)
                    v.tensor_tensor(at, at, banks[n].rearrange("p (c k) -> p k c", c=4), ALU.add).then_inc(sem("x3_ready"), 1)

            dve.wait_ge(sem("x3_ready"), C // 4)

            def take_logits(n, u):
                dve.wait_ge(sem("lg4_done"), n + 1)
                v.tensor_copy(logits[:, bass.ds(KB * n, KB), :], zp[u][:, 0:KB * E8].rearrange("p (k e) -> p k e", e=E8)
                              ).then_inc(sem("lg4_ready"), 1)

            def router(turn, u):
                n = 2 * turn + u
                o = Order(dve, sem("dve_router"), n, 1 + STAT_LINKS + RSQRT_LINKS)
                for k in range(KB):
                    last = v.bn_stats(st_r[:, k, :], xt[:, bass.ds(KB * n + k, 1), :])
                o.link(last)
                token_stats(v, o, st_r, ln_mean[:, bass.ds(KB * n, KB)], var_r, rst_r, 1e-5, KB)
                last = rsqrt(v, o, var_r, rsi_r.bitcast(I32), rst_r,
                             lambda t, y: v.scalar_tensor_tensor(out=ln_rstd[:, bass.ds(KB * n, KB)], in0=t,
                                                                 scalar=1.5, in1=y, op0=ALU.add, op1=ALU.mult))
                last.then_inc(sem("rstd_r"), 1)
                dve.wait_ge(sem("rstd_r"), n + 1)
                if not (isinstance(turn, int) and turn == 0):
                    dve.wait_ge(sem("tn4_done"), n - 1)
                for k in range(KB):
                    last = v.tensor_scalar(tn4[u][:, k, :], flat(xt[:, bass.ds(KB * n + k, 1), :]),
                                           ln_mean[:, bass.ds(KB * n + k, 1)], ln_rstd[:, bass.ds(KB * n + k, 1)],
                                           ALU.subtract, ALU.mult)
                last.then_inc(sem("tn4_ready"), 1)
                if not (isinstance(turn, int) and turn == 0 and u == 0):
                    take_logits(n - 1, 1 - u)
                o.end()

            for u in range(2):
                router(0, u)
            with dve.Fori(1, NBLK // KB // 2) as turn:
                for u in range(2):
                    router(turn, u)
            take_logits(NBLK // KB - 1, 1)

            for r in (2, 3):
                route(r)
                with dve.Fori(0, GB // 2) as turn:
                    for u in range(2):
                        make_pieces(r, turn, u)

            per = CT // QT

            def last_bias(pair):
                for n in range(2 * per):
                    Q, u, s = 2 * per * pair + n, n % 2, n // per
                    dve.wait_ge(sem("yq_done"), Q + 1)
                    if n >= 2 or not isinstance(pair, int):
                        dve.wait_ge(sem(f"yq_out{(n - 2) % per}"), 64 * (2 * pair + (n - 2) // per + 1))
                    v.tensor_tensor(y_quad[u], zp[u][:, :].rearrange("p (q c) -> p q c", q=QT),
                                    fb2[s].rearrange("p (a c) -> p a c", a=1).to_broadcast([P, QT, P]), ALU.add
                                    ).then_inc(sem("yq_ready"), 1)

            repeat(dve, 0, E8 // 2, last_bias)

            def final_sum(turn, u):
                n = 2 * turn + u
                o = Order(dve, sem("dve_final"), n, 1)
                dve.wait_ge(sem(f"yf_in{u}"), 16 * (turn + 1))
                if not (isinstance(turn, int) and turn == 0):
                    dve.wait_ge(sem("fin_t_done"), n - 1)
                for k in range(KC):
                    last = v.scalar_tensor_tensor(out=fin[u][:, k, :], in0=y_fin[u][:, k, 0, :],
                                                  scalar=weight[:, 0, bass.ds(KC * n + k, 1)],
                                                  in1=flat(xt[:, bass.ds(KC * n + k, 1), :]), op0=ALU.mult, op1=ALU.add)
                o.link(last)
                for k in range(KC):
                    last = v.scalar_tensor_tensor(out=fin[u][:, k, :], in0=y_fin[u][:, k, 1, :],
                                                  scalar=weight[:, 1, bass.ds(KC * n + k, 1)],
                                                  in1=fin[u][:, k, :], op0=ALU.mult, op1=ALU.add)
                last.then_inc(sem("fin_ready"), 1)
                o.end()

            for u in range(2):
                final_sum(0, u)
            with dve.Fori(1, NBLK // 8) as turn:
                for u in range(2):
                    final_sum(turn, u)


_INS = ['x', 'L0_conv_se_w1', 'L0_conv_se_b1', 'L0_conv_se_w2', 'L0_conv_se_b2', 'L0_conv_down_w', 'L0_conv_gus',
        'L0_ffn_Wg', 'L0_ffn_W1', 'L0_ffn_W2', 'L0_ffn_W3', 'L0_ffn_b3', 'L1_conv_codebook', 'L1_conv_bias',
        'L1_ffn_gate_w', 'L1_ffn_w1', 'L1_ffn_b1', 'L1_ffn_w2', 'L1_ffn_b2']


def kernel(**inputs):
    import numpy as _np
    import concourse.bacc as _bacc
    from concourse import mybir as _mybir
    from concourse.bass_utils import run_bass_kernel_spmd as _run

    nc = _bacc.Bacc("TRN2", target_bir_lowering=False, num_devices=1)
    shapes = {'x': (B, C, HW), 'L0_conv_gus': (HW, HW)}
    arrays, args = {}, []
    for name in _INS:
        a = _np.ascontiguousarray(inputs[name])
        a = a.reshape(shapes.get(name, a.shape))
        arrays[f"in_{name}"] = a
        args.append(nc.dram_tensor(f"in_{name}", a.shape, _mybir.dt.from_np(a.dtype), kind="ExternalInput").ap())
    args.append(nc.dram_tensor("out", (B, C, HW), F32, kind="ExternalOutput").ap())
    metaformer(nc, *args)
    r = _run(nc, [arrays], core_ids=[0])
    return r.results[0]["out"].reshape(B, C, IMG, IMG)
```

```python
from contextlib import ExitStack

import concourse.bass as bass
from concourse import mybir

F32 = mybir.dt.float32
I32 = mybir.dt.int32
U32 = mybir.dt.uint32
ALU = mybir.AluOpType
ACT = mybir.ActivationFunctionType
AX_X = mybir.AxisListType.X
P = 128


class Order:

    def __init__(self, eng, sem, visit, per, before=0):
        self.eng, self.sem, self.base, self.per, self.k = eng, sem, before + visit * per, per, 0

    def step(self, ins):
        ins.then_inc(self.sem, 1)
        self.k += 1

    def settle(self):
        self.eng.wait_ge(self.sem, self.base + self.k)

    def link(self, ins):
        self.step(ins)
        self.settle()

    def end(self):
        assert self.k == self.per, (self.sem, self.k, self.per)


RSQRT_LINKS = 10


def rsqrt(v, order, x, y_int, tmp, out_ins, begin=True, end=True):
    y = y_int.bitcast(F32)
    if begin:
        order.link(v.tensor_scalar(y_int, x.bitcast(I32), 1, None, ALU.arith_shift_right))
        order.link(v.tensor_scalar(y_int, y_int, -1, 0x5F3759DF, ALU.mult, ALU.add))
    for n in range(0 if begin else 1, 3 if end else 1):
        order.link(v.scalar_tensor_tensor(out=tmp, in0=y, scalar=-0.5, in1=y, op0=ALU.mult, op1=ALU.mult))
        order.link(v.tensor_tensor(tmp, tmp, x, ALU.mult))
        if n < 2:
            order.link(v.scalar_tensor_tensor(out=y, in0=tmp, scalar=1.5, in1=y, op0=ALU.add, op1=ALU.mult))
    return out_ins(tmp, y) if end else None


class Arena:

    def __init__(self, tensor, words):
        self.tensor, self.words, self.at = tensor, words, 0

    def take(self, *shape, parts=P):
        n = 1
        for s in shape:
            n *= s
        ap = self.tensor[0:parts, self.at:self.at + n]
        self.at += n
        assert self.at <= self.words, ("SBUF is full", self.at, self.words)
        if len(shape) == 2:
            ap = ap.rearrange("p (a b) -> p a b", a=shape[0])
        elif len(shape) == 3:
            ap = ap.rearrange("p (a b c) -> p a b c", a=shape[0], b=shape[1])
        return ap


def repeat(eng, first, last, body):
    body(first)
    with eng.Fori(first + 1, last) as turn:
        body(turn)


STAT_LINKS = 7


def token_stats(v, order, st, mean, var, tmp, eps, n):
    even, odd, even2, odd2 = (st[:, 0:n, c] for c in (1, 4, 2, 5))
    order.step(v.tensor_tensor(mean, even, odd, ALU.add))
    order.step(v.tensor_tensor(tmp, even, odd, ALU.subtract))
    order.link(v.tensor_tensor(var, even2, odd2, ALU.add))
    order.step(v.tensor_scalar(mean, mean, 0.5, None, ALU.mult))
    order.link(v.tensor_tensor(tmp, tmp, tmp, ALU.mult))
    order.link(v.scalar_tensor_tensor(out=var, in0=tmp, scalar=P / 4, in1=var, op0=ALU.mult, op1=ALU.add))
    order.link(v.tensor_scalar(var, var, 1.0 / P, eps, ALU.mult, ALU.add))


B, C, HW = 16, 128, 1024
IMG = 32
NBLK = B * HW // P
KB = HW // P
PAIRS = B // 2
E8 = 8
WIN = 6 * IMG
XS_W = 132
HALO = HW + 2 * IMG

GROUPS = 2
GB = NBLK // GROUPS
F0 = 384
FC0 = F0 // P
RING = 8
TILES0 = -(-(2 * GB + E8 - 1) // RING) * RING
F1 = 512
FC1 = F1 // P
CAP = -(-5 * B * HW // (4 * E8))
CT = CAP // P
assert CT * P == CAP
DVE_SHARE = 3
EARLY = 5
BESIDE = 4
ROUTE_BESIDE = 6
QT = 4
ROW_W = 132
NOWHERE = 1 << 20
TOKENS = B * HW
KER = 7
CODES = 1024
CG = 8
NCG = C // CG
EDGE = KER // 2
DX = 2 * IMG - 1


def code_place(kh, kw):
    inverse = pow(1337 % CODES, -1, CODES)
    return (kh * 7919 + kw * 2971 + 3 * 104729) * inverse % CODES


def metaformer(nc, x, se_w1, se_b1, se_w2, se_b2, down_w, gus, moe_wg, moe_w1, moe_w2, moe_w3, moe_b3,
               codebook, conv_bias, gate_w, ffn_w1, ffn_b1, ffn_w2, ffn_b2, out):
    hid = se_w1.shape[0]
    with ExitStack() as ctx:
        sems = {}

        def sem(name):
            if name not in sems:
                sems[name] = ctx.enter_context(nc.semaphore(name))
            return sems[name]

        WORDS = 53200
        arena = Arena(ctx.enter_context(nc.sbuf_tensor("arena", [P, WORDS], F32)), WORDS)
        tp = [ctx.enter_context(nc.psum_tensor(f"tp{i}", [P, 1024], F32)) for i in range(2)]
        zp = [ctx.enter_context(nc.psum_tensor(f"zp{i}", [P, 512], F32)) for i in range(2)]
        gp = [ctx.enter_context(nc.psum_tensor(f"gp{i}", [P, 512], F32)) for i in range(2)]

        xt = arena.take(NBLK, P)
        idle = arena.take(2)
        ident = arena.take(P)
        ones = arena.take(P)
        upper = arena.take(P)
        logits = arena.take(NBLK, E8)
        ln_mean = arena.take(NBLK)
        ln_rstd = arena.take(NBLK)
        ln_var = arena.take(16)
        rs_int = arena.take(16)
        rs_tmp = arena.take(16)
        moe_wg_s = arena.take(E8)
        gate_s = arena.take(E8)
        prefer = arena.take(E8)
        cap_base = arena.take(E8)
        carry = arena.take(E8)
        taken = arena.take(E8)
        n_tiles = arena.take(E8)
        first_slot = arena.take(E8)
        tile_no = arena.take(TILES0)
        tile_expert = [arena.take(TILES0) for _ in range(GROUPS)]
        slot = arena.take(2, NBLK)
        weight = arena.take(2, NBLK)
        row_id = arena.take(2, NBLK)
        fill = arena.take(ROW_W)
        piece = arena.take(4, ROW_W)
        piece_slot = arena.take(4)
        routing = arena.at
        top = arena.take(4, GB)
        e_hot = arena.take(2, GB, E8)
        e_tmp = arena.take(3, GB, E8)
        phase = arena.at
        wg = arena.take(8, KB, P)
        w2t = arena.take(P)
        mask = arena.take(6, IMG)
        npad = arena.take(KB)
        w1t_se = arena.take(hid)
        w2t_se = arena.take(P)
        b1_se = arena.take(1)
        b2_se = arena.take(1)
        hidden = arena.take(2)
        xsum = arena.take(2)
        gatey = arena.take(2)
        xs = [arena.take(2, KB, XS_W) for _ in range(2)]
        xc = arena.take(2, HW)
        sig = arena.take(2, HALO)
        ee = arena.take(KB, WIN)
        g2n = arena.take(KB, P)
        g2r = [arena.take(2, 8, P) for _ in range(2)]
        zz = [arena.take(2, HW) for _ in range(2)]
        xr = arena.take(HW)
        tn = arena.take(KB, P)
        tnc = xr.rearrange("p (k c) -> p k c", k=KB)
        st = arena.take(16, 6)
        mean_f = arena.take(16)
        rstd_f = arena.take(16)
        zst = arena.take(4, 6)
        zmv = arena.take(2, 2)
        zsc = arena.take(2)
        znm = arena.take(2)
        rden = arena.take(KB)
        centred = arena.take(2, P)
        t32 = arena.take(8)
        arena.at = phase
        m1_s = arena.take(E8 * F0)
        m3_s = arena.take(E8 * F0)
        tile_in = [arena.take(ROW_W) for _ in range(RING)]
        act_t = [arena.take(FC0, P) for _ in range(2)]
        assert arena.at <= phase + NBLK // 2 * P
        arena.at = phase + NBLK * P
        m2_s = arena.take(E8, FC0, P)
        b3_s = arena.take(E8 * F0)
        tok_t = [arena.take(P) for _ in range(2)]
        act_h = [arena.take(F0) for _ in range(2)]
        act_g = [arena.take(F0) for _ in range(2)]
        y_tile = [arena.take(P) for _ in range(RING)]
        mean_2, rstd_2 = arena.take(2 * KB), arena.take(2 * KB)
        mean_c, rstd_c = ([z[:, KB * u:KB * (u + 1)] for u in range(2)] for z in (mean_2, rstd_2))
        var_c = arena.take(2 * KB)
        st_c = arena.take(2 * KB, 6)
        rsi_c = arena.take(2 * KB)
        rst_c = arena.take(2 * KB)
        toep = [arena.take(12, IMG, CG)]
        conv_b = arena.take(P)
        arena.at = phase
        xn = arena.take(NBLK, P)
        toep.append(arena.take(12, IMG, CG))
        y_in8 = [arena.take(KB, 2, P) for _ in range(2)]
        arena.at = routing
        y_in = [arena.take(KB // 2, 2, P) for _ in range(2)]
        arena.at = phase
        piece_more = arena.take(4, ROW_W)
        more_slot = arena.take(4)
        tn4 = [arena.take(KB, P) for _ in range(2)]
        tnc4 = [arena.take(KB, P) for _ in range(2)]
        fw1 = [arena.take(F1) for _ in range(2)]
        fw2 = [arena.take(FC1, P) for _ in range(2)]
        fb1 = [arena.take(FC1) for _ in range(2)]
        fb2 = [arena.take(P) for _ in range(2)]
        quad_in = [arena.take(QT, ROW_W) for _ in range(CT // QT)]
        quad_t = [arena.take(QT * P) for _ in range(2)]
        hid_t = [arena.take(FC1, QT * P) for _ in range(2)]
        y_quad = [arena.take(QT, P) for _ in range(2)]
        y_fin = [arena.take(KB // 2, 2, P) for _ in range(2)]
        fin = [arena.take(KB // 2, P) for _ in range(2)]
        fin_t = [arena.take(KB // 2 * P) for _ in range(2)]
        ln_shift = arena.take(NBLK)
        var_r = arena.take(2 * KB)
        st_r = arena.take(2 * KB, 6)
        rsi_r = arena.take(2 * KB)
        rst_r = arena.take(2 * KB)

        def piece_of(q):
            return (piece[:, q:q + 1, :], piece_slot[:, q:q + 1]) if q < 4 else (piece_more[:, q - 4:q - 3, :], more_slot[:, q - 4:q - 3])

        def sent(r, turn, q):
            halves = GB // 2
            if r < 2:
                return r * halves + turn
            return (2 * halves if q < 4 else 0) + (r - 2) * (halves // 2) + turn // 2

        def scratch(name, *shape):
            return nc.dram_tensor(name, shape, F32, kind="Internal").ap()

        slots = [scratch(f"slots_{g}", TILES0 * P, ROW_W) for g in range(GROUPS)] + [scratch("slots_cap", E8 * CAP, ROW_W)]
        results = scratch("results", 2 * TOKENS, P)
        codes = scratch("codes", CODES + P)
        by_dist = scratch("by_dist", NCG, KER, DX, CG)
        taps = scratch("taps", NCG, IMG, KER, IMG, CG)
        code_idx = piece[:, 0, 0:8]
        code_val = piece[:, 0, 8:16]
        tap_w = piece[0:KER * KER, 1, 0:P]
        tap_sign = piece[0:KER * KER, 2, 0:P]
        gus_s = xt[:, 0:8 * KB, :].rearrange("p (j k) c -> p j (k c)", j=8)
        dw_s = xt[:, 64:66, :].rearrange("p a b -> p (a b)")
        w1t = xt[:, 66, :]

        banks = [tp[0][:, 0:512], tp[0][:, 512:1024], tp[1][:, 0:512], tp[1][:, 512:1024],
                 zp[0][:, :], zp[1][:, :], gp[0][:, :], gp[1][:, :]]

        block = ctx.enter_context(nc.Block())

        def pipeline(eng, visit, route=None, aside=None):
            visit(0, 0, True, False, False)
            if aside is not None:
                aside(0)
            visit(1, 1, True, True, False)
            if aside is not None:
                aside(1)
            with eng.Fori(1, 3) as turn:
                visit(2 * turn, 0, True, True, True)
                visit(2 * turn + 1, 1, True, True, True)
            if route is not None:
                route(0)
            visit(6, 0, True, True, True)
            visit(7, 1, True, True, True)
            visit(PAIRS, 0, False, True, True)
            visit(PAIRS + 1, 1, False, False, True)
            if route is not None:
                route(1)

        @block.sync
        def _(sp):
            ld = lambda dst, src: sp.dma_start(dst, src, allow_slow_non_contiguous=True).then_inc(sem("const_in"), 16)
            sp.dma_start(xc, x[0:2].rearrange("b c p -> c b p")).then_inc(sem("x_in"), 16)
            ld(dw_s, down_w)
            sp.dma_start(gus_s, gus.rearrange("(a j) q -> a j q", j=8)).then_inc(sem("gus_in"), 16)
            ld(w1t_se, se_w1.rearrange("h c -> c h"))
            ld(w2t_se[0:hid, :], se_w2.rearrange("c h -> h c"))
            ld(b1_se[0:hid, :], se_b1.rearrange("(h a) -> h a", a=1))
            ld(b2_se, se_b2.rearrange("(h a) -> h a", a=1))
            ld(moe_wg_s, moe_wg)

            ld(gate_s, gate_w.rearrange("e c -> c e"))
            def aside(n):
                if n == 0:
                    sp.wait_ge(sem("pool_const"), 1)
                    sp.dma_start(by_dist.rearrange("g y x c -> (g y x c)").rearrange("(p a w) -> p a w", p=P, a=KER),
                                 fill[:, 0:DX].rearrange("p (a w) -> p a w", a=1).to_broadcast([P, KER, DX])
                                 ).then_inc(sem("taps_zero"), 16)
                    sp.wait_ge(sem("codes_in"), 16 * (CODES // P))
                    sp.dma_start(codes[0:CODES].rearrange("(a p) -> p a", p=P), code_val, allow_slow_non_contiguous=True
                                 ).then_inc(sem("codes_out"), 16)
                    sp.dma_start(codes[CODES:CODES + P].rearrange("(p a) -> p a", a=1), code_val[:, 0:1],
                                 allow_slow_non_contiguous=True).then_inc(sem("codes_out"), 16)
                    sp.wait_ge(sem("codes_out"), 32)
                    for row in range(KER * KER):
                        at = code_place(KER - 1 - row // KER, KER - 1 - row % KER)
                        sp.dma_start(tap_w[row:row + 1, :], codes[at:at + P].rearrange("(a c) -> a c", a=1)
                                     ).then_inc(sem("tapw_in"), 16)
                else:
                    sp.wait_ge(sem("tapw_ready"), 1)
                    sp.wait_ge(sem("taps_zero"), 16)
                    for dy in range(KER):
                        sp.dma_start(by_dist[:, dy, IMG - 1 - EDGE:IMG + EDGE, :].rearrange("g x c -> x g c"),
                                     tap_w[KER * dy:KER * dy + KER, :].rearrange("p (g c) -> p g c", c=CG)
                                     ).then_inc(sem("dist_out"), 16)

            def fill_slots(m, first, rows):
                sp.dma_start(slots[m].rearrange("(p r) w -> p r w", p=P)[:, bass.ds(first, rows), :],
                             fill.rearrange("p (a w) -> p a w", a=1).to_broadcast([P, rows, ROW_W])
                             ).then_inc(sem(f"fill_out{m}"), 16)

            def visit(i, s, front, mid, back):
                def residual(picture):
                    sp.dma_start(xr, x[bass.ds(picture, 1)].rearrange("b c p -> c (b p)")).then_inc(sem("res_in"), 16)

                if back:
                    sp.wait_ge(sem("x1_ready"), 2 * (i - 2) + 1)
                    residual(2 * (i - 2) + 1)
                if front and not (isinstance(i, int) and i == PAIRS - 1):
                    sp.wait_ge(sem("f1_done"), 2 * i + 2)
                    sp.dma_start(xc, x[bass.ds(2 * i + 2, 2)].rearrange("b c p -> c b p")).then_inc(sem("x_in"), 16)
                if (back or (isinstance(i, int) and i == 1)) and not (isinstance(i, int) and i == PAIRS + 1):
                    if back:
                        sp.wait_ge(sem("x1_ready"), 2 * (i - 2) + 2)
                        sp.wait_ge(sem("lg_done"), 2 * (i - 2) + 2)
                    residual(2 * (i - 1))
                if front:
                    for b in range(2):
                        for k in range(KB):
                            sp.wait_ge(sem("g2_ready"), 4 * (2 * i + b) + k // 2 + 1)
                            sp.dma_start(g2r[s][16 * k:16 * k + 16, b].rearrange("a j c -> a j c"), g2n[:, k, :]
                                         ).then_inc(sem("g2r_in"), 16)
                if isinstance(i, int) and i == PAIRS + 1:
                    sp.wait_ge(sem("z_ready"), 8 * PAIRS)
                    for dst, src in ((m1_s, moe_w1), (m3_s, moe_w3)):
                        sp.dma_start(dst.rearrange("p (e f) -> p e f", e=E8), src.rearrange("e d f -> d e f")
                                     ).then_inc(sem("moe_in"), 16)
                if back:
                    m = int(isinstance(i, int))
                    if not (isinstance(i, int) and i == PAIRS + 1):
                        fill_slots(m, (i - 2 - 4 * m) * (TILES0 // 4), TILES0 // 4)

            pipeline(sp, visit, aside=aside)

            sp.wait_ge(sem("lg_ready"), PAIRS)
            sp.dma_start(m2_s, moe_w2.rearrange("e (c f) d -> f e c d", f=P)).then_inc(sem("moe_in"), 16)
            sp.dma_start(b3_s, moe_b3.rearrange("(a e) f -> a (e f)", a=1).partition_broadcast(P)).then_inc(sem("moe_in"), 16)
            fill_slots(1, TILES0 // 4 * 3, TILES0 // 4)
            sp.wait_ge(sem("dist_out"), 16 * KER)
            for col in range(IMG):
                sp.dma_start(taps[:, col].rearrange("g y x c -> g y (x c)"),
                             by_dist[:, :, IMG - 1 - col:DX - col, :].rearrange("g y x c -> g y (x c)")
                             ).then_inc(sem("taps_out"), 16)
            turns = TILES0 // RING

            def load_tiles(g, turn):
                for q in range(RING):
                    sp.wait_ge(sem(f"y_out{q}"), 16 * (g * turns + turn))
                    sp.dma_start(tile_in[q], slots[g][bass.ds((turn * RING + q) * P, P), :]
                                 ).then_inc(sem(f"tile_in{q}"), 16)

            rows = E8 * CT // (turns - 1)
            by_token = results.rearrange("(k p s) c -> p k (s c)", p=P, s=2)

            def load_results(dst, name, n, u):
                blocks = dst[u].shape[1]
                sp.dma_start(dst[u].rearrange("p k s c -> p k (s c)"), by_token[:, bass.ds(blocks * n, blocks), :]
                             ).then_inc(sem(f"{name}{u}"), 16)

            def load_toep(g):
                if g >= 2:
                    sp.wait_ge(sem("conv_done"), CG // 4 * (g - 1))
                for y in range(4):
                    src = taps[g].rearrange("i a x c -> i a (x c)")
                    sp.dma_start(toep[g % 2][IMG * y:IMG * y + IMG, y + 1:y + 1 + KER].rearrange("p a x c -> p a (x c)"), src
                                 ).then_inc(sem(f"toep_in{g % 2}"), 16)

            for q in range(4):
                sp.wait_ge(sem(f"piece_out{q}"), 16 * (GB // 2))
            repeat(sp, 0, turns, lambda turn: load_tiles(0, turn))
            for q in range(4):
                sp.wait_ge(sem(f"piece_out{q}"), 16 * (GB // 2) * 2)
            sp.dma_start(conv_b, conv_bias.rearrange("(a c) -> a c", a=1).partition_broadcast(P)).then_inc(sem("convb_in"), 16)
            sp.wait_ge(sem("taps_out"), 16 * IMG)
            sp.wait_ge(sem("toep_zero"), 1)
            load_toep(0)
            sp.wait_ge(sem("weighed"), 2)

            def beside(turn, u):
                if isinstance(turn, int):
                    for q in range(RING if turn == 0 else 0):
                        sp.wait_ge(sem(f"y_out{q}"), 16 * turns)
                else:
                    sp.wait_ge(sem("x2_ready"), turn - 1)
                if not (isinstance(turn, int) and turn == 0):
                    load_results(y_in, "y_in", turn, u)
                load_tiles(1, turn)
                if isinstance(turn, int) and turn == 0:
                    load_results(y_in, "y_in", turn, u)
                fill_slots(2, rows * turn, rows)

            for u in range(2):
                beside(u, u)
            with sp.Fori(1, turns // 2) as turn:
                for u in range(2):
                    beside(2 * turn + u, u)
            load_tiles(1, turns - 1)

            for q in range(RING):
                sp.wait_ge(sem(f"y_out{q}"), 16 * turns * GROUPS)
            for u in range(2):
                load_results(y_in8, "y_in", KB + u, u)
            with sp.Fori(KB // 2 + 1, KB) as turn:
                for u in range(2):
                    sp.wait_ge(sem("x2_ready"), KB + 2 * turn + u - 1)
                    load_results(y_in8, "y_in", 2 * turn + u, u)
            sp.wait_ge(sem("toep_zero"), 2)
            load_toep(1)
            for g in range(2, NCG):
                load_toep(g)

            sp.wait_ge(sem("x3_ready"), C // 4)

            def load_expert(e, s):
                for dst, src in ((fw1[s], ffn_w1[bass.ds(e, 1)].rearrange("e d f -> d (e f)")),
                                 (fw2[s], ffn_w2[bass.ds(e, 1)].rearrange("e (c f) d -> f (e c) d", f=P)),
                                 (fb1[s], ffn_b1[bass.ds(e, 1)].rearrange("e (c f) -> f (e c)", f=P)),
                                 (fb2[s], ffn_b2[bass.ds(e, 1)].partition_broadcast(P))):
                    sp.dma_start(dst, src, allow_slow_non_contiguous=True).then_inc(sem(f"expert_in{s}"), 16)

            load_expert(0, 0)
            load_expert(1, 1)
            for q in range(8):
                sp.wait_ge(sem(f"piece_out{q}"), 16 * sent(3, GB // 2, q))
            per = CT // QT

            def load_quads(pair, s):
                for m in range(per):
                    sp.wait_ge(sem(f"yq_out{m}"), 64 * (2 * pair + s))
                    sp.dma_start(quad_in[m], slots[2][bass.ds((2 * per * pair + per * s + m) * QT * P, QT * P), :]
                                 .rearrange("(q p) w -> p q w", p=P)).then_inc(sem(f"quad_in{m}"), 16)

            load_quads(0, 0)
            load_quads(0, 1)
            with sp.Fori(1, E8 // 2) as pair:
                for s in range(2):
                    sp.wait_ge(sem("yq_ready"), per * (2 * pair - 1 + s))
                    load_expert(2 * pair + s, s)
                    load_quads(pair, s)

            for m in range(per):
                sp.wait_ge(sem(f"yq_out{m}"), 64 * E8)
            for u in range(2):
                load_results(y_fin, "yf_in", u, u)
            with sp.Fori(1, NBLK // 8) as turn:
                for u in range(2):
                    sp.wait_ge(sem("fin_ready"), 2 * turn + u - 1)
                    load_results(y_fin, "yf_in", 2 * turn + u, u)

        @block.gpsimd
        def _(pool):
            g = nc.gpsimd
            n = [0]

            def link(ins):
                n[0] += 1
                ins.then_inc(sem("pool_own"), 1)
                pool.wait_ge(sem("pool_own"), n[0])

            g.memset(ident, 0.0)
            g.memset(idle, 0.0)
            g.memset(ones, 1.0)
            g.memset(fill, 0.0)
            g.memset(carry, 0.0)
            link(g.memset(piece.rearrange("p a b -> p (a b)"), 0.0))
            link(g.iota(code_idx.bitcast(I32), pattern=[[P * 1337 % CODES, 8]], base=0, channel_multiplier=1337 % CODES))
            g.iota(fill[:, P:P + 1].bitcast(I32), pattern=[[0, 1]], base=NOWHERE, channel_multiplier=0)
            for k in range(2):
                g.iota(row_id[:, k, :].bitcast(I32), pattern=[[2 * P, NBLK]], base=k, channel_multiplier=2)
            exact = dict(allow_small_or_imprecise_dtypes=True)
            g.iota(prefer, pattern=[[-1, E8]], base=E8, channel_multiplier=0, **exact)
            g.iota(cap_base, pattern=[[CAP, E8]], base=0, channel_multiplier=0, **exact)
            g.iota(tile_no, pattern=[[1, TILES0]], base=0, channel_multiplier=0, **exact)
            link(g.iota(tap_sign.bitcast(I32), pattern=[[1, P]], base=0, channel_multiplier=1))
            g.memset(t32[:, 6:7], 0.0).then_inc(sem("iotas"), 1)
            g.memset(mask.rearrange("p a b -> p (a b)"), 0.0)
            g.memset(npad, 3.0)
            for s in range(2):
                g.memset(xs[s][:, :, :, P:P + 1], 1.0)
            g.memset(sig[:, :, 0:IMG], 0.0)
            link(g.memset(sig[:, :, HALO - IMG:HALO], 0.0))
            link(g.affine_select(out=ident, in_=ident, compare_op=ALU.not_equal, fill=1.0, base=0,
                                 pattern=[[-1, P]], channel_multiplier=1))
            link(g.affine_select(out=upper, in_=ones, compare_op=ALU.is_gt, fill=0.0, base=0,
                                 pattern=[[1, P]], channel_multiplier=-1))
            for y in range(4):
                band = mask[IMG * y:IMG * y + IMG, y:y + 3, :]
                one = ones[IMG * y:IMG * y + IMG, 0:96].rearrange("p (a b) -> p a b", a=3)
                link(g.affine_select(out=band, in_=one, compare_op=ALU.is_ge, fill=0.0, base=1,
                                     pattern=[[0, 3], [-1, IMG]], channel_multiplier=1))
                link(g.affine_select(out=band, in_=band, compare_op=ALU.is_ge, fill=0.0, base=1,
                                     pattern=[[0, 3], [1, IMG]], channel_multiplier=-1))
            g.memset(npad[0:IMG, 0:1], 2.0)
            link(g.memset(npad[P - IMG:P, KB - 1:KB], 2.0))
            link(g.iota(t32[:, 0:1].bitcast(I32), pattern=[[0, 1]], base=0, channel_multiplier=1))
            g.memset(t32[:, 4:5], 0.0).then_inc(sem("pool_const"), 1)
            pool.wait_ge(sem("code_idx"), 1)
            for a in range(CODES // P):
                g.indirect_dma_start(code_val[:, a:a + 1], None, codebook.rearrange("(n a) -> n a", a=1),
                                     bass.IndirectOffsetOnAxis(ap=code_idx[:, a:a + 1].bitcast(U32), axis=0),
                                     bounds_check=CODES - 1, oob_is_err=False).then_inc(sem("codes_in"), 16)

            def alone(name, count):
                pool.wait_ge(sem(name), count)
                if not isinstance(count, int):
                    pool.sem_inc(sem("passed"), 1)

            def send(r, q, turn):
                row, place = piece_of(q)
                g.indirect_dma_start(slots[min(r, 2)], bass.IndirectOffsetOnAxis(ap=place.bitcast(U32), axis=0),
                                     row[:, 0, :], None, bounds_check=slots[min(r, 2)].shape[0] - 1, oob_is_err=False
                                     ).then_inc(sem(f"piece_out{q}"), 16)

            pool.wait_ge(sem("fill_out0"), 16 * 4)
            pool.wait_ge(sem("dist_out"), 16 * KER)
            pool.wait_ge(sem("slots_ready"), 1)

            def first_rows(turn):
                blks = bass.ds(2 * turn, 2)
                wide = lambda z: z.rearrange("p (b c) -> p b c", c=1).to_broadcast([P, 2, P])
                g.tensor_tensor(centred, xt[:, blks, :], wide(ln_mean[:, blks]), ALU.subtract
                                ).then_inc(sem("rows_own"), 1)
                pool.wait_ge(sem("rows_own"), 3 * turn + 1)
                for b in range(2):
                    blk = bass.ds(2 * turn + b, 1)
                    both = slice(2 * b, 2 * b + 2)
                    if not isinstance(turn, int):
                        for q in (2 * b, 2 * b + 1):
                            pool.wait_ge(sem(f"piece_out{q}"), 16 * turn)
                    g.tensor_tensor(piece[:, both, 0:P], centred[:, b:b + 1, :].to_broadcast([P, 2, P]),
                                    ln_rstd[:, blk].rearrange("p (b c) -> p b c", c=1).to_broadcast([P, 2, P]), ALU.mult)
                    g.tensor_copy(piece[:, both, P:P + 1].bitcast(I32), row_id[:, :, blk].bitcast(I32))
                    g.tensor_copy(piece_slot[:, both].rearrange("p (k a) -> p k a", a=1).bitcast(I32),
                                  slot[:, :, blk].bitcast(I32)).then_inc(sem("rows_own"), 1)
                    alone("rows_own", 3 * turn + 2 + b)
                    for q in (2 * b, 2 * b + 1):
                        send(0, q, turn)

            repeat(pool, 0, GB // 2, first_rows)

            def result_out(visit, q):
                alone("y_ready", RING * visit + q + 1)
                g.indirect_dma_start(results, bass.IndirectOffsetOnAxis(ap=tile_in[q][:, P:P + 1].bitcast(U32), axis=0),
                                     y_tile[q], None, bounds_check=2 * TOKENS - 1, oob_is_err=False
                                     ).then_inc(sem(f"y_out{q}"), 16)

            def piece_out(r, turn, q):
                if q % 2 == 0:
                    alone(f"pieces_made{q // 2 % 2}", (r - 1) * (GB // 2) + turn + 1)
                send(r, q, turn)

            turns = TILES0 // RING
            pool.wait_ge(sem("fill_out1"), 16 * 4)
            pool.wait_ge(sem("slots_ready"), 2)
            g.memset(toep[0].rearrange("p a b c -> p (a b c)"), 0.0).then_inc(sem("toep_zero"), 1)
            with pool.Fori(0, 2 * GB // RING) as turn:
                for q in range(RING):
                    piece_out(1, RING // 4 * turn + q // 4, q % 4)
                    result_out(turn, q)
            for visit in range(2 * GB // RING, turns):
                for q in range(RING):
                    result_out(visit, q)
            with pool.Fori(turns, 2 * turns) as visit:
                for q in range(RING):
                    result_out(visit, q)

            pool.wait_ge(sem("y_ready"), GROUPS * TILES0)
            g.memset(toep[1].rearrange("p a b c -> p (a b c)"), 0.0).then_inc(sem("toep_zero"), 1)

            pool.wait_ge(sem("convb_in"), 16)
            def add_bias(n, chunks):
                alone("xn3_ready", chunks)
                part = xt[:, bass.ds(KB * n, KB), :]
                g.tensor_tensor(part, part, conv_b.rearrange("p (a c) -> p a c", a=1).to_broadcast([P, KB, P]), ALU.add
                                ).then_inc(sem("biased"), 1)

            with pool.Fori(0, KB) as n:
                add_bias(n, 2 * n + 2)
            with pool.Fori(KB, 2 * KB) as n:
                add_bias(n, n + KB + 1)

            pool.wait_ge(sem("fill_out2"), 16 * (TILES0 // RING - 1))
            for r in (2, 3):
                with pool.Fori(0, GB // 4) as turn:
                    for q in range(8):
                        piece_out(r, 2 * turn + q // 4, q)
            per = CT // QT
            with pool.Fori(0, E8 // 2) as pair:
                for n in range(2 * per):
                    m, u = n % per, n % 2
                    alone("yq_ready", 2 * per * pair + n + 1)
                    for q in range(QT):
                        g.indirect_dma_start(results, bass.IndirectOffsetOnAxis(ap=quad_in[m][:, q, P:P + 1].bitcast(U32), axis=0),
                                             y_quad[u][:, q, :], None, bounds_check=2 * TOKENS - 1, oob_is_err=False
                                             ).then_inc(sem(f"yq_out{m}"), 16)

        @block.tensor
        def _(pe):
            t = nc.tensor
            pe.wait_ge(sem("pool_const"), 1)
            pe.wait_ge(sem("const_in"), 16 * 7)
            t.transpose(gp[0][:, 0:P], dw_s[:, 0:P], ident)
            t.transpose(gp[0][:, P:2 * P], dw_s[:, P:2 * P], ident).then_inc(sem("wt_done"), 1)
            pe.wait_ge(sem("w1t_ready"), 1)
            pe.wait_ge(sem("gus_in"), 16)
            for j in range(8):
                dst = tp[j % 2]
                if j >= 2:
                    pe.wait_ge(sem("wg_ready"), j - 1)
                for k in range(KB):
                    m = t.matmul(dst[:, P * k:P * k + P], gus_s[:, j, P * k:P * k + P], w1t, start=True, stop=True)
                m.then_inc(sem("wg_done"), 1)
            pe.wait_ge(sem("wg_ready"), 8)

            def visit(i, s, front, mid, back):
                c = 1 - s

                def product(j):
                    if not mid:
                        return
                    if not (isinstance(i, int) and i == 1 and j < 2):
                        pe.wait_ge(sem("z_ready"), 8 * (i - 1) + j - 1)
                    dst = zp[j % 2][:, 0:2 * P].rearrange("p (b c) -> p b c", b=2)
                    for k in range(KB):
                        t.matmul(dst, wg[:, j, k, :], xs[c][:, :, k, 0:P], start=(k == 0), stop=False)
                    if j == 0:
                        pe.wait_ge(sem("g2r_in"), 256 * i)
                    t.matmul(dst, w2t, g2r[c][:, :, j, :], start=False, stop=True).then_inc(sem("z_done"), 1)

                product(0)
                product(1)
                if isinstance(i, int) and i == 6:
                    ranks(0)
                if front:
                    pe.wait_ge(sem("x_in"), 16 * (i + 1))
                    if not (isinstance(i, int) and i == 0):
                        pe.wait_ge(sem("exp_ready"), 8 * i)
                    for b in range(2):
                        for k in range(KB):
                            m = t.transpose(tp[b][:, P * k:P * k + P], xc[:, b, P * k:P * k + P], ident)
                        m.then_inc(sem("f1_done"), 1)
                product(2)
                if back:
                    for b in range(2):
                        pe.wait_ge(sem("x1_ready"), 2 * (i - 2) + b + 1)
                        if front:
                            pe.wait_ge(sem("xs_out"), 2 * i + b + 1)
                        elif isinstance(i, int):
                            pe.wait_ge(sem("exp_ready"), 8 * PAIRS)
                            if i > PAIRS:
                                pe.wait_ge(sem("tnc_ready"), 2 * (PAIRS - 1))
                        for k in range(KB):
                            m = t.transpose(tp[b][:, P * k:P * k + P], zz[s][:, b, P * k:P * k + P], ident)
                        m.then_inc(sem("d1_done"), 1)
                product(3)
                if front:
                    for b in range(2):
                        pe.wait_ge(sem("xn_ready"), 2 * i + b + 1)
                        if back:
                            pe.wait_ge(sem("xt_ready"), 2 * (i - 2) + b + 1)
                        else:
                            pe.wait_ge(sem("xs_out"), 2 * i + b + 1)
                        for k in range(KB):
                            m = t.transpose(tp[b][:, P * k:P * k + P], xs[s][:, b, k, 0:P], ident)
                        m.then_inc(sem("f2_done"), 1)
                product(4)
                if front:
                    pe.wait_ge(sem("xnc_ready"), 2 * i + 2)
                    if not (isinstance(i, int) and i == 0):
                        pe.wait_ge(sem("g2_ready"), 8 * i)
                    if isinstance(i, int) and i == 6:
                        pe.wait_ge(sem("ranks_read"), 1)
                    t.matmul(gp[0][0:hid, 0:2], w1t_se, xsum, start=True, stop=True).then_inc(sem("se1_done"), 1)
                product(5)
                if back:
                    for b in range(2):
                        pe.wait_ge(sem("tn_ready"), 2 * (i - 2) + b + 1)
                        if not front:
                            pe.wait_ge(sem("xt_ready"), 2 * (i - 2) + b + 1)
                        for k in range(KB):
                            m = t.transpose(tp[b][:, P * k:P * k + P], tn[:, k, :], ident)
                        m.then_inc(sem("d3_done"), 1)
                if front:
                    pe.wait_ge(sem("hid_ready"), i + 1)
                    t.matmul(gp[0][:, 8:10], w2t_se[0:hid, :], hidden[0:hid, :], start=True, stop=True
                             ).then_inc(sem("se2_done"), 1)
                if back:
                    for b in range(2):
                        pe.wait_ge(sem("tnc_ready"), 2 * (i - 2) + b + 1)
                        if b == 0 and isinstance(i, int) and i > PAIRS:
                            pe.wait_ge(sem("lg_ready"), i - 2)
                        if not front:
                            pe.wait_ge(sem("g2_ready"), 8 * PAIRS)
                        for k in range(KB):
                            m = t.matmul(gp[1][:, 256 + E8 * (KB * b + k):256 + E8 * (KB * b + k + 1)], tnc[:, k, :],
                                         moe_wg_s, start=True, stop=True)
                        m.then_inc(sem("lg_done"), 1)
                if front:
                    pe.wait_ge(sem("gate_ready"), i + 1)
                    if back:
                        pe.wait_ge(sem("lg_ready"), i - 1)
                    for b in range(2):
                        m = t.matmul(gp[1][:, P * b:P * b + P], gatey[:, b:b + 1].to_broadcast([P, P]), ident,
                                     start=True, stop=True)
                    m.then_inc(sem("gb_done"), 1)
                    if back:
                        pe.wait_ge(sem("tnc_ready"), 2 * (i - 2) + 2)
                    for b in range(2):
                        pe.wait_ge(sem("sig_ready"), 2 * i + b + 1)
                        if b == 1:
                            pe.wait_ge(sem("exp_ready"), 8 * i + 4)
                        for k in range(KB):
                            m = t.matmul(tp[k // 4][:, 256 * (k % 4):256 * (k % 4) + WIN],
                                         sig[:, b, IMG + P * k:IMG + P * k + P], sig[:, b, P * k:P * k + WIN],
                                         start=True, stop=True)
                            if k % 2:
                                m.then_inc(sem("gram_done"), 1)
                        product(6 + b)
                        if b == 0:
                            pe.wait_ge(sem("xs_ready"), i + 1)
                        for kk in range(4):
                            pe.wait_ge(sem("ee_ready"), 4 * (2 * i + b) + min(4, kk + 2))
                            if b or kk >= 2:
                                pe.wait_ge(sem("g2_ready"), 4 * (2 * i + b) + kk - 1)
                            for k in (2 * kk, 2 * kk + 1):
                                dst = gp[kk % 2][:, 256 * (k % 2):256 * (k % 2) + P + 1]
                                rhs = xs[s][:, b, k, 0:P + 1]
                                m = t.matmul(dst, ee[:, k, IMG:IMG + P], rhs, start=True, stop=True)
                                if k:
                                    m = t.matmul(dst[0:IMG], ee[96:P, k - 1, IMG + P:WIN], xs[s][96:P, b, k - 1, 0:P + 1],
                                                 start=False, stop=True, skip_group_check=True, tile_position=(96, 0))
                                if k < KB - 1:
                                    m = t.matmul(dst[96:P], ee[0:IMG, k + 1, 0:IMG], xs[s][0:IMG, b, k + 1, 0:P + 1],
                                                 start=False, stop=True, skip_group_check=True, tile_position=(0, 96))
                            m.then_inc(sem("at_done"), 1)
                else:
                    product(6)
                    product(7)

            def ranks(r):
                pe.wait_ge(sem("picked"), r + 1)
                if r < 2:
                    pe.wait_ge(sem("g2_ready"), (48, 64)[r])
                    pe.wait_ge(sem("lg_ready"), (4, 8)[r])
                else:
                    pe.wait_ge(sem("ranks_read"), r)
                mask_r = e_tmp[:, 2].rearrange("p k e -> p (k e)")
                t.matmul(gp[0][:, :], upper, mask_r, start=True, stop=True)
                t.matmul(gp[1][:, :], ones, mask_r, start=True, stop=True).then_inc(sem("ranked"), 1)

            pipeline(pe, visit)
            ranks(1)

            turns = TILES0 // RING
            pe.wait_ge(sem("moe_in"), 64)
            pe.wait_ge(sem("ranks_read"), 2)

            experts_kept = [pe.alloc_register(f"expert_kept{n}") for n in range(3)]

            def expert_tiles(g):
                te = tile_expert[g].bitcast(I32)

                def up(turn, q, first=False):
                    T = g * TILES0 + RING * turn + q
                    pe.wait_ge(sem(f"tile_in{q}"), 16 * (g * turns + turn + 1))
                    if not (g == 0 and first):
                        pe.wait_ge(sem("tok_t_ready"), T)
                    t.transpose(gp[0][:, 0:P], tile_in[q][:, 0:P], ident).then_inc(sem("tok_t_done"), 1)

                def down_1(T, u):
                    pe.wait_ge(sem("act_ready"), T + 1)
                    for c in range(FC0):
                        m = t.transpose(zp[u][:, P * c:P * c + P], act_h[u][:, P * c:P * c + P], ident)
                    m.then_inc(sem("act_t_done"), 1)

                def down_2(n, u, e):
                    T = g * TILES0 + n
                    pe.wait_ge(sem("act_t_ready"), T + 1)
                    if not (g == 0 and isinstance(n, int) and n < 2):
                        pe.wait_ge(sem("y_ready"), T - 1)
                    for c in range(FC0):
                        m = t.matmul(tp[1][:, 512 * u + F0:512 * u + F0 + P], act_t[u][:, c, :], m2_s[:, bass.ds(e, 1), c, :],
                                     start=(c == 0), stop=(c == FC0 - 1))
                    m.then_inc(sem("y_done"), 1)

                def expert(n):
                    return pe.value_load(te[0:1, bass.ds(n, 1)], min_val=0, max_val=E8 - 1)

                def stretch(turn, first, last):
                    e = ([None, None, expert(0)] if first else
                         [pe.snap(kept, min_val=0, max_val=E8 - 1) for kept in experts_kept])
                    for j in range(RING):
                        n, u = RING * turn + j, j % 2
                        T = g * TILES0 + n
                        pe.wait_ge(sem("tok_t_ready"), T + 1)
                        t.matmul(tp[0][:, 512 * u:512 * u + F0], tok_t[u], m1_s[:, bass.ds(e[2] * F0, F0)], start=True, stop=True
                                 ).then_inc(sem("h_done"), 1)
                        e_next = expert(n + 1) if not (last and j == RING - 1) else None
                        if not (last and j == RING - 1):
                            up(turn + (j + 1) // RING, (j + 1) % RING)
                        if not (first and j < 2):
                            down_2(n - 2, u, e[0])
                        if not (first and j == 0):
                            down_1(T - 1, 1 - u)
                        t.matmul(tp[1][:, 512 * u:512 * u + F0], tok_t[u], m3_s[:, bass.ds(e[2] * F0, F0)], start=True, stop=True
                                 ).then_inc(sem("g_done"), 1)
                        e = [e[1], e[2], e_next]
                    if not last:
                        for kept, value in zip(experts_kept, e):
                            pe.reg_mov(kept, value)
                    else:
                        down_1(T, u)
                        down_2(n - 1, 1 - u, e[0])
                        down_2(n, u, e[1])

                up(0, 0, first=True)
                stretch(0, True, False)
                with pe.Fori(1, turns - 1) as turn:
                    stretch(turn, False, False)
                stretch(turns - 1, False, True)

            for g in range(GROUPS):
                pe.wait_ge(sem("slots_ready"), g + 1)
                expert_tiles(g)

            pe.wait_ge(sem("xn3_ready"), 3 * KB)
            pe.wait_ge(sem("y_ready"), GROUPS * TILES0)

            def channels(turn):
                for n in range(8):
                    s, cc = (n // 2) % 2, 4 * (n % 2)
                    if n % 2 == 0:
                        pe.wait_ge(sem(f"toep_in{s}"), 64 * (2 * turn + n // 4 + 1))
                    if not isinstance(turn, int):
                        pe.wait_ge(sem("x3_ready"), 8 * turn)
                    for c in range(4):
                        chan = 32 * turn + 4 * n + c
                        dst = banks[n][:, P * c:P * c + P]
                        src = xn[:, :, bass.ds(chan, 1)].rearrange("p k c -> p (k c)")
                        w = toep[s].rearrange("p a x c -> p (a x) c")
                        t.matmul(dst, w[:, P:2 * P, cc + c], src, start=True, stop=True)
                        dk, sk = (z.rearrange("p (b k) -> p b k", b=B) for z in (dst, src))
                        t.matmul(dk[:, :, 0:KB - 1], w[:, 0:P, cc + c], sk[:, :, 1:KB], start=False, stop=True,
                                 skip_group_check=True)
                        m = t.matmul(dk[:, :, 1:KB], w[:, 2 * P:3 * P, cc + c], sk[:, :, 0:KB - 1], start=False, stop=True,
                                     skip_group_check=True)
                    m.then_inc(sem("conv_done"), 1)

            repeat(pe, 0, NCG // 4, channels)

            pe.wait_ge(sem("x3_ready"), C // 4)

            def router(turn):
                for u in range(2):
                    n = 2 * turn + u
                    pe.wait_ge(sem("tn4_ready"), n + 1)
                    pe.wait_ge(sem("tn4_rest"), n + 1)
                    if not isinstance(turn, int):
                        pe.wait_ge(sem("tnc4_ready"), 2 * turn)
                    for k in range(KB):
                        m = t.transpose(tp[u][:, P * k:P * k + P], tn4[u][:, k, :], ident)
                    m.then_inc(sem("tn4_done"), 1)
                for u in range(2):
                    pe.wait_ge(sem("tnc4_ready"), 2 * turn + u + 1)
                    if not isinstance(turn, int):
                        pe.wait_ge(sem("lg4_ready"), 2 * turn)
                    for k in range(KB):
                        m = t.matmul(zp[u][:, E8 * k:E8 * k + E8], tnc4[u][:, k, :], gate_s, start=True, stop=True)
                    m.then_inc(sem("lg4_done"), 1)

            repeat(pe, 0, EARLY, router)
            ranks(2)
            with pe.Fori(EARLY, NBLK // KB // 2) as turn:
                router(turn)
            ranks(3)

            per = CT // QT

            def quad_up(pair, n, first=False):
                Q, m = 2 * per * pair + n, n % per
                pe.wait_ge(sem(f"quad_in{m}"), 16 * (2 * pair + n // per + 1))
                if not first:
                    pe.wait_ge(sem("quad_t_ready"), Q)
                for q in range(QT):
                    last = t.transpose(gp[0][:, P * q:P * q + P], quad_in[m][:, q, 0:P], ident)
                last.then_inc(sem("quad_t_done"), 1)

            def quad_down(Q, u, s):
                pe.wait_ge(sem("hid_t_ready"), 4 * Q + 4)
                for q in range(QT):
                    for c in range(FC1):
                        m = t.matmul(zp[u][:, P * q:P * q + P], hid_t[u][:, c, P * q:P * q + P], fw2[s][:, c, :],
                                     start=(c == 0), stop=(c == FC1 - 1))
                m.then_inc(sem("yq_done"), 1)

            def expert_pair(pair, first, last):
                for n in range(2 * per):
                    Q, u, s = 2 * per * pair + n, n % 2, n // per
                    if n % per == 0:
                        pe.wait_ge(sem(f"expert_in{s}"), 64 * (pair + 1))
                    pe.wait_ge(sem("quad_t_ready"), Q + 1)
                    for c in range(FC1):
                        if not (first and n == 0):
                            pe.wait_ge(sem("hid_t_ready"), 4 * (Q - 1) + c + 1)
                        t.matmul(tp[c // 2][:, 512 * (c % 2):512 * (c % 2) + 512], fw1[s][:, P * c:P * c + P], quad_t[u],
                                 start=True, stop=True).then_inc(sem("hq_done"), 1)
                        if c == 1 and not (last and n == 2 * per - 1):
                            quad_up(pair if n < 2 * per - 1 else pair + 1, (n + 1) % (2 * per))
                    if not (first and n == 0):
                        if not (first and n < 3):
                            pe.wait_ge(sem("yq_ready"), Q - 2)
                        quad_down(Q - 1, 1 - u, ((n - 1) // per) % 2)
                if last:
                    pe.wait_ge(sem("yq_ready"), Q - 1)
                    quad_down(Q, u, s)

            pe.wait_ge(sem("ranks_read"), 4)
            quad_up(0, 0, first=True)
            expert_pair(0, True, False)
            with pe.Fori(1, E8 // 2 - 1) as pair:
                expert_pair(pair, False, False)
            expert_pair(E8 // 2 - 1, False, True)

            pe.wait_ge(sem("yq_ready"), E8 * CT // QT)

            def output(turn):
                for u in range(2):
                    pe.wait_ge(sem("fin_ready"), 2 * turn + u + 1)
                    if not isinstance(turn, int):
                        pe.wait_ge(sem("fin_t_ready"), 2 * turn)
                    for k in range(KB // 2):
                        m = t.transpose(tp[u][:, P * k:P * k + P], fin[u][:, k, :], ident)
                    m.then_inc(sem("fin_t_done"), 1)

            repeat(pe, 0, NBLK // 8, output)

        @block.scalar
        def _(act):
            A = nc.scalar.activation

            def visit(i, s, front, mid, back):
                def z_out(j):
                    if mid:
                        act.wait_ge(sem("z_done"), 8 * (i - 1) + j + 1)
                        A(zz[1 - s][:, :, P * j:P * j + P], zp[j % 2][:, 0:2 * P].rearrange("p (b c) -> p b c", b=2),
                          ACT.Copy).then_inc(sem("z_ready"), 1)

                if back:
                    for b in range(2):
                        act.wait_ge(sem("zsc_ready"), i - 1)
                        A(zz[s][:, b, :], zz[s][:, b, :], ACT.Identity, bias=znm[:, b:b + 1], scale=zsc[:, b:b + 1]
                          ).then_inc(sem("zn_ready"), 1)
                if front:
                    for b in range(2):
                        act.wait_ge(sem("f1_done"), 2 * i + b + 1)
                        if b == 0 and not (isinstance(i, int) and i < 2):
                            act.wait_ge(sem("z_done"), 8 * (i - 1))
                        A(xs[s][:, b, :, 0:P], tp[b][:, :].rearrange("p (k c) -> p k c", k=KB), ACT.Copy
                          ).then_inc(sem("xs_out"), 1)
                z_out(0)
                z_out(1)
                if back:
                    for b in range(2):
                        act.wait_ge(sem("d1_done"), 2 * (i - 2) + b + 1)
                        A(xt[:, bass.ds(2 * KB * (i - 2) + KB * b, KB), :], tp[b][:, :].rearrange("p (k c) -> p k c", k=KB),
                          ACT.Copy).then_inc(sem("xt_ready"), 1)
                        z_out(2 + b)
                else:
                    z_out(2)
                    z_out(3)
                if front:
                    for b in range(2):
                        act.wait_ge(sem("f2_done"), 2 * i + b + 1)
                        if not (isinstance(i, int) and i == 0):
                            act.wait_ge(sem("gram_done"), 8 * i)
                        A(sig[:, b, IMG:IMG + HW], tp[b][:, :], ACT.Copy, accum_out=xsum[:, b:b + 1]
                          ).then_inc(sem("xnc_ready"), 1)
                z_out(4)
                if front:
                    act.wait_ge(sem("se1_done"), i + 1)
                    A(hidden[0:hid, :], gp[0][0:hid, 0:2], ACT.Relu, bias=b1_se[0:hid, :], scale=1.0 / HW
                      ).then_inc(sem("hid_ready"), 1)
                if back:
                    for b in range(2):
                        act.wait_ge(sem("d3_done"), 2 * (i - 2) + b + 1)
                        if b:
                            act.wait_ge(sem("lg_done"), 2 * (i - 2) + b)
                        elif isinstance(i, int) and i > PAIRS:
                            act.wait_ge(sem("lg_done"), 2 * (i - 2))
                        A(tnc, tp[b][:, :].rearrange("p (k c) -> p k c", k=KB), ACT.Copy).then_inc(sem("tnc_ready"), 1)
                        if b == 0:
                            z_out(5)
                else:
                    z_out(5)
                if front:
                    act.wait_ge(sem("se2_done"), i + 1)
                    A(gatey, gp[0][:, 8:10], ACT.Sigmoid, bias=b2_se).then_inc(sem("gate_ready"), 1)
                    for b in range(2):
                        if b == 0:
                            act.wait_ge(sem("gate_ready"), i + 1)
                        A(sig[:, b, IMG:IMG + HW], sig[:, b, IMG:IMG + HW], ACT.Sigmoid, scale=gatey[:, b:b + 1]
                          ).then_inc(sem("sig_ready"), 1)
                    for b in range(2):
                        for kk in range(4):
                            act.wait_ge(sem("gram_done"), 4 * (2 * i + b) + kk + 1)
                            if kk == 0 and b:
                                act.wait_ge(sem("at_done"), 8 * i + 4)
                            elif kk == 0 and not (isinstance(i, int) and i == 0):
                                act.wait_ge(sem("at_done"), 8 * i)
                            src = tp[kk // 2][:, 512 * (kk % 2):512 * (kk % 2) + 512].rearrange("p (a w) -> p a w", a=2)
                            A(ee[:, 2 * kk:2 * kk + 2, :], src[:, :, 0:WIN], ACT.Exp, scale=1.0 / C
                              ).then_inc(sem("exp_ready"), 1)
                        z_out(6 + b)
                else:
                    z_out(6)
                    z_out(7)

            def weights(r):
                act.wait_ge(sem("gap"), r + 1)
                part = slice(GB * (r % 2), GB * (r % 2) + GB)
                A(weight[:, 0, part], top[:, 2, :], ACT.Sigmoid)
                A(weight[:, 1, part], top[:, 2, :], ACT.Sigmoid, scale=-1.0).then_inc(sem("weighed"), 1)

            pipeline(act, visit, weights)

            turns = TILES0 // RING

            def hidden_out(T, u):
                act.wait_ge(sem("h_done"), T + 1)
                A(act_h[u], tp[0][:, 512 * u:512 * u + F0], ACT.Silu).then_inc(sem("silu_ready"), 1)

            def act_t_out(T, u):
                act.wait_ge(sem("act_t_done"), T + 1)
                A(act_t[u].rearrange("p a b -> p (a b)"), zp[u][:, 0:F0], ACT.Copy).then_inc(sem("act_t_ready"), 1)

            def tok_t_out(T, u):
                act.wait_ge(sem("tok_t_done"), T + 1)
                A(tok_t[u], gp[0][:, 0:P], ACT.Copy).then_inc(sem("tok_t_ready"), 1)

            def turn_tiles(g, turn, first, last, beside=None):
                for q in range(RING):
                    T, u = g * TILES0 + RING * turn + q, q % 2
                    if not (last and q == RING - 1):
                        tok_t_out(T + 1, 1 - u)
                    if not (first and q == 0):
                        act_t_out(T - 1, 1 - u)
                    hidden_out(T, u)
                    if beside is not None and q < KB // 2:
                        normalise(*beside, q)
                if last:
                    act_t_out(T, u)

            def normalise(n, u, k, blocks=KB // 2, before=0):
                if k == 0:
                    act.wait_ge(sem("stats3"), before + n + 1)
                flat = lambda z: z.rearrange("p a c -> p (a c)")
                blk = blocks * n + k
                place = blk + NBLK // 2 if before == 0 else blk - NBLK // 2
                done = A(flat(xn[:, bass.ds(place, 1), :]), flat(xt[:, bass.ds(blk, 1), :]), ACT.Identity,
                         bias=mean_c[u][:, k:k + 1], scale=rstd_c[u][:, k:k + 1])
                if k == blocks - 1:
                    done.then_inc(sem("xn3_ready"), 1)

            tok_t_out(0, 0)
            turn_tiles(0, 0, True, False)
            with act.Fori(1, turns - 1) as turn:
                turn_tiles(0, turn, False, False)
            turn_tiles(0, turns - 1, False, True)
            tok_t_out(TILES0, 0)
            turn_tiles(1, 0, True, False)
            turn_tiles(1, 1, False, False, beside=(0, 0))
            with act.Fori(1, turns // 2) as turn:
                for v in range(2):
                    turn_tiles(1, 2 * turn + v, False, False, beside=(2 * turn + v - 1, 1 - v))
            turn_tiles(1, turns - 1, False, True, beside=(turns - 2, 1))

            def weigh_second(turn):
                for u in range(2):
                    act.wait_ge(sem(f"y_in{u}"), 16 * (KB // 2 + turn + 1))
                    for k in range(KB):
                        y = y_in8[u][:, k, 1, :]
                        done = A(y, y, ACT.Copy, scale=weight[:, 1, bass.ds(KB * (2 * turn + u) + k, 1)])
                    done.then_inc(sem("y_weighed"), 1)

            def normalise_two(turn):
                for u in range(2):
                    for k in range(KB):
                        normalise(2 * turn + u, u, k, blocks=KB, before=KB)

            weigh_second(KB // 2)
            with act.Fori(KB // 2 + 1, KB) as turn:
                weigh_second(turn)
                normalise_two(turn - 1)
            normalise_two(KB - 1)

            def router(turn):
                act.wait_ge(sem("stats4"), turn + 1)
                for u in range(2):
                    n = 2 * turn + u
                    if not isinstance(turn, int):
                        act.wait_ge(sem("tn4_done"), n - 1)
                    for k in range(DVE_SHARE, KB):
                        blk = bass.ds(KB * n + k, 1)
                        last = A(tn4[u][:, k, :], xt[:, blk, :].rearrange("p a c -> p (a c)"), ACT.Identity,
                                 bias=ln_shift[:, blk], scale=ln_rstd[:, blk])
                    last.then_inc(sem("tn4_rest"), 1)
                for u in range(2):
                    act.wait_ge(sem("tn4_done"), 2 * turn + u + 1)
                    if not isinstance(turn, int):
                        act.wait_ge(sem("lg4_done"), 2 * turn)
                    A(tnc4[u].rearrange("p a b -> p (a b)"), tp[u][:, :], ACT.Copy).then_inc(sem("tnc4_ready"), 1)

            repeat(act, 0, EARLY, router)
            weights(2)
            with act.Fori(EARLY, NBLK // KB // 2) as turn:
                router(turn)
            weights(3)

            per = CT // QT

            def quad_t_out(Q, u):
                act.wait_ge(sem("quad_t_done"), Q + 1)
                A(quad_t[u], gp[0][:, :], ACT.Copy).then_inc(sem("quad_t_ready"), 1)

            def gelu_pair(pair, last):
                for n in range(2 * per):
                    Q, u, s = 2 * per * pair + n, n % 2, n // per
                    for c in range(FC1):
                        act.wait_ge(sem("hq_done"), 4 * Q + c + 1)
                        A(hid_t[u][:, c, :], tp[c // 2][:, 512 * (c % 2):512 * (c % 2) + 512], ACT.Gelu,
                          bias=fb1[s][:, c:c + 1]).then_inc(sem("hid_t_ready"), 1)
                        if c == 1 and not (last and n == 2 * per - 1):
                            quad_t_out(Q + 1, 1 - u)

            quad_t_out(0, 0)
            with act.Fori(0, E8 // 2 - 1) as pair:
                gelu_pair(pair, False)
            gelu_pair(E8 // 2 - 1, True)

            def output(turn):
                for u in range(2):
                    n = 2 * turn + u
                    act.wait_ge(sem("fin_t_done"), n + 1)
                    if not isinstance(turn, int):
                        act.wait_ge(sem(f"out_done{u}"), 16 * turn)
                    A(fin_t[u], tp[u][:, 0:512], ACT.Copy).then_inc(sem("fin_t_ready"), 1)
                    act.wait_ge(sem("fin_t_ready"), n + 1)
                    act.dma_start(out[bass.ds(turn, 1), :, 512 * u:512 * u + 512].rearrange("b c p -> c (b p)"), fin_t[u]
                                  ).then_inc(sem(f"out_done{u}"), 16)

            repeat(act, 0, NBLK // 8, output)
            for u in range(2):
                act.wait_ge(sem(f"out_done{u}"), 16 * (NBLK // 8))

        @block.vector
        def _(dve):
            v = nc.vector
            cst = Order(dve, sem("dve_const"), 0, 10)
            dve.wait_ge(sem("iotas"), 1)
            v.tensor_scalar(code_idx.bitcast(I32), code_idx.bitcast(I32), CODES - 1, None, ALU.bitwise_and
                            ).then_inc(sem("code_idx"), 1)
            dve.wait_ge(sem("pool_const"), 1)
            ti = t32[:, 0:1].bitcast(I32)
            cst.link(v.tensor_scalar(ti, ti, IMG - 1, None, ALU.bitwise_and))
            cst.link(v.tensor_copy(t32[:, 1:2], ti))
            cst.link(v.tensor_scalar(t32[:, 2:3], t32[:, 1:2], 0.0, None, ALU.is_equal))
            cst.link(v.tensor_scalar(t32[:, 3:4], t32[:, 1:2], float(IMG - 1), None, ALU.is_equal))
            cst.link(v.tensor_tensor(t32[:, 2:3], t32[:, 2:3], t32[:, 3:4], ALU.add))
            cst.link(v.tensor_scalar(t32[:, 2:3], t32[:, 2:3], -1.0, 3.0, ALU.mult, ALU.add))
            cst.link(v.tensor_scalar(npad, npad, t32[:, 2:3], None, ALU.mult))
            cst.link(v.tensor_scalar(npad, npad, -1.0, 9.0, ALU.mult, ALU.add))
            dve.wait_ge(sem("wt_done"), 1)
            cst.link(v.tensor_copy(w2t, gp[0][:, P:2 * P]))
            v.tensor_copy(w1t, gp[0][:, 0:P]).then_inc(sem("w1t_ready"), 1)
            cst.step(v.memset(t32[:, 5:6], 0.0))
            cst.end()
            for j in range(8):
                dve.wait_ge(sem("wg_done"), j + 1)
                v.tensor_copy(wg[:, j].rearrange("p k c -> p (k c)"), tp[j % 2][:, :]).then_inc(sem("wg_ready"), 1)

            def visit(i, s, front, mid, back):
                if back:
                    o = Order(dve, sem("dve_zstat"), i - 2, 16)
                    dve.wait_ge(sem("z_ready"), 8 * (i - 1))
                    for b in range(2):
                        for h in range(2):
                            o.step(v.bn_stats(zst[:, 2 * b + h, :], zz[s][:, b, 512 * h:512 * h + 512]))
                    o.settle()
                    o.step(v.memset(t32[:, 5:6], 0.0))
                    for b in range(2):
                        last = v.bn_aggr(zmv[:, b, :], zst[:, 2 * b:2 * b + 2, :])
                    o.link(last)
                    v.tensor_scalar(ln_var[:, 0:2], zmv[:, :, 1], 1e-5, None, ALU.add).then_inc(sem("zvar"), 1)
                    dve.wait_ge(sem("zvar"), i - 1)
                    last = rsqrt(v, o, ln_var[:, 0:2], rs_int[:, 0:2].bitcast(I32), rs_tmp[:, 0:2],
                                 lambda t, y: v.scalar_tensor_tensor(out=zsc, in0=t, scalar=1.5, in1=y,
                                                                     op0=ALU.add, op1=ALU.mult))
                    last.then_inc(sem("zsc_own"), 1)
                    dve.wait_ge(sem("zsc_own"), i - 1)
                    v.scalar_tensor_tensor(out=znm, in0=zmv[:, :, 0], scalar=-1.0, in1=zsc, op0=ALU.mult, op1=ALU.mult
                                           ).then_inc(sem("zsc_ready"), 1)
                    o.end()
                    for b in range(2):
                        dve.wait_ge(sem("zn_ready"), 2 * (i - 2) + b + 1)
                        v.scalar_tensor_tensor(out=zz[s][:, b, :], in0=zz[s][:, b, :], scalar=0.2, in1=zz[s][:, b, :],
                                               op0=ALU.mult, op1=ALU.max).then_inc(sem("leaky"), 1)
                        dve.wait_ge(sem("leaky"), 2 * (i - 2) + b + 1)
                        dve.wait_ge(sem("res_in"), 16 * (2 * (i - 2) + b + 1))
                        v.tensor_tensor(zz[s][:, b, :], zz[s][:, b, :], xr, ALU.add).then_inc(sem("x1_ready"), 1)
                if front:
                    for b in range(2):
                        dve.wait_ge(sem("xs_out"), 2 * i + b + 1)
                        for k in range(KB):
                            last = v.bn_stats(st[:, KB * b + k, :], xs[s][:, b, k, 0:P])
                    o = Order(dve, sem("dve_front"), i, 2 + STAT_LINKS + RSQRT_LINKS)
                    o.link(last)
                    token_stats(v, o, st, mean_f, ln_var, rs_tmp, 1e-6, 2 * KB)
                    last = rsqrt(v, o, ln_var, rs_int.bitcast(I32), rs_tmp,
                                 lambda t, y: v.scalar_tensor_tensor(out=rstd_f, in0=t, scalar=1.5, in1=y,
                                                                     op0=ALU.add, op1=ALU.mult))
                    o.link(last)
                    for b in range(2):
                        for k in range(KB):
                            w = xs[s][:, b, k, 0:P]
                            last = v.tensor_scalar(w, w, mean_f[:, KB * b + k:KB * b + k + 1], rstd_f[:, KB * b + k:KB * b + k + 1],
                                                   ALU.subtract, ALU.mult)
                        last.then_inc(sem("xn_ready"), 1)
                    o.end()
                if back:
                    o = Order(dve, sem("dve_back"), i - 2, 2 + STAT_LINKS + RSQRT_LINKS)
                    blk = 2 * KB * (i - 2)
                    blks = bass.ds(blk, 2 * KB)
                    for b in range(2):
                        dve.wait_ge(sem("xt_ready"), 2 * (i - 2) + b + 1)
                        for k in range(KB):
                            last = v.bn_stats(st[:, KB * b + k, :], xt[:, bass.ds(blk + KB * b + k, 1), :])
                    o.link(last)
                    token_stats(v, o, st, ln_mean[:, blks], ln_var, rs_tmp, 1e-5, 2 * KB)
                    last = rsqrt(v, o, ln_var, rs_int.bitcast(I32), rs_tmp,
                                 lambda t, y: v.scalar_tensor_tensor(out=ln_rstd[:, blks], in0=t,
                                                                     scalar=1.5, in1=y, op0=ALU.add, op1=ALU.mult))
                    o.link(last)
                    for b in range(2):
                        if b:
                            dve.wait_ge(sem("d3_done"), 2 * (i - 2) + b)
                        for k in range(KB * b, KB * b + KB):
                            last = v.tensor_scalar(tn[:, k % KB, :], xt[:, bass.ds(blk + k, 1), :].rearrange("p a c -> p (a c)"),
                                                   ln_mean[:, bass.ds(blk + k, 1)], ln_rstd[:, bass.ds(blk + k, 1)],
                                                   ALU.subtract, ALU.mult)
                        last.then_inc(sem("tn_ready"), 1)
                    o.end()
                    dve.wait_ge(sem("lg_done"), 2 * (i - 2) + 2)
                    v.tensor_copy(logits[:, bass.ds(2 * KB * (i - 2), 2 * KB), :],
                                  gp[1][:, 256:256 + 2 * KB * E8].rearrange("p (k e) -> p k e", e=E8)
                                  ).then_inc(sem("lg_ready"), 1)
                if front:
                    dve.wait_ge(sem("gb_done"), i + 1)
                    dve.wait_ge(sem("f2_done"), 2 * i + 2)
                    for b in range(2):
                        gb = gp[1][:, P * b:P * b + P].rearrange("p (a c) -> p a c", a=1).to_broadcast([P, KB, P])
                        last = v.tensor_tensor(xs[s][:, b, :, 0:P], xs[s][:, b, :, 0:P], gb, ALU.mult)
                    last.then_inc(sem("xs_ready"), 1)
                    for b in range(2):
                        for kk in range(4):
                            dve.wait_ge(sem("exp_ready"), 4 * (2 * i + b) + kk + 1)
                            mk = mask.rearrange("p a b -> p (a b)").rearrange("p (a w) -> p a w", a=1).to_broadcast([P, 2, WIN])
                            v.tensor_tensor(ee[:, 2 * kk:2 * kk + 2, :], ee[:, 2 * kk:2 * kk + 2, :], mk, ALU.mult
                                            ).then_inc(sem("ee_ready"), 1)
                        if b:
                            dve.wait_ge(sem("g2r_in"), 128 * (2 * i + b))
                        elif not (isinstance(i, int) and i == 0):
                            dve.wait_ge(sem("g2r_in"), 256 * i)
                        o = Order(dve, sem("dve_g2"), 2 * i + b, 8)
                        if b or not (isinstance(i, int) and i == 0):
                            dve.wait_ge(sem("g2_ready"), 4 * (2 * i + b))
                        for kk in range(4):
                            dve.wait_ge(sem("at_done"), 4 * (2 * i + b) + kk + 1)
                            src = gp[kk % 2][:, :].rearrange("p (a w) -> p a w", a=2)
                            rd = rden[:, 2 * kk:2 * kk + 2]
                            o.link(v.tensor_tensor(rd, src[:, :, P], npad[:, 2 * kk:2 * kk + 2], ALU.add))
                            o.link(v.reciprocal(rd, rd))
                            v.tensor_tensor(g2n[:, 2 * kk:2 * kk + 2, :], src[:, :, 0:P],
                                            rd.rearrange("p (a c) -> p a c", c=1).to_broadcast([P, 2, P]), ALU.mult
                                            ).then_inc(sem("g2_ready"), 1)
                        o.end()

            def aside(n):
                if n == 1:
                    o = Order(dve, sem("dve_taps"), 0, 3)
                    ti = tap_sign.bitcast(I32)
                    o.link(v.tensor_scalar(ti, ti, 1, None, ALU.bitwise_and))
                    o.link(v.tensor_copy(tap_sign, ti))
                    o.link(v.tensor_scalar(tap_sign, tap_sign, 2.0, -1.0, ALU.mult, ALU.add))
                    o.end()
                    dve.wait_ge(sem("tapw_in"), 16 * KER * KER)
                    v.tensor_tensor(tap_w, tap_w, tap_sign, ALU.mult).then_inc(sem("tapw_ready"), 1)

            route_links = [0]

            def route(r, beside=lambda j: None):
                o = Order(dve, sem("dve_route"), 1, route_links[-1])
                half = slice(GB * (r % 2), GB * (r % 2) + GB)
                wide = lambda z: z.rearrange("p (k e) -> p k e", e=1).to_broadcast([P, GB, E8])
                per_e = lambda z: z.rearrange("p (k e) -> p k e", k=1).to_broadcast([P, GB, E8])
                best, second, gap, pick = (top[:, n, :] for n in range(4))
                work, place, both = (e_tmp[:, n] for n in range(3))
                lg = logits[:, half, :]
                dve.wait_ge(sem("lg_ready" if r < 2 else "lg4_ready"), (4, 8, 8, 16)[r])
                if r:
                    dve.wait_ge(sem("weighed"), r)

                def first_of(value, src, hot):
                    o.link(v.tensor_reduce(value, src, AX_X, ALU.max))
                    o.link(v.tensor_tensor(work, src, wide(value), ALU.is_equal))
                    o.link(v.tensor_tensor(work, work, per_e(prefer), ALU.mult))
                    o.link(v.tensor_reduce(pick, work, AX_X, ALU.max))
                    o.link(v.tensor_tensor(hot, work, wide(pick), ALU.is_equal))

                first_of(best, lg, e_hot[:, 0])
                beside(0)
                o.link(v.scalar_tensor_tensor(out=both, in0=e_hot[:, 0], scalar=-3.0e38, in1=lg, op0=ALU.mult, op1=ALU.add))
                first_of(second, both, e_hot[:, 1])
                beside(1)
                v.tensor_tensor(gap, best, second, ALU.subtract).then_inc(sem("gap"), 1)
                v.tensor_tensor(both, e_hot[:, 0], e_hot[:, 1], ALU.add).then_inc(sem("picked"), 1)

                beside(2)
                dve.wait_ge(sem("ranked"), r + 1)
                sums = work.rearrange("p k e -> p (k e)").rearrange("p (e k) -> p e k", e=E8)
                rank, count = (z[:, :].rearrange("p (k e) -> p k e", e=E8) for z in gp)
                for e in range(E8):
                    last = v.tensor_tensor_scan(sums[:, e, :], ones[:, 0:GB], count[:, :, e], 0.0, ALU.mult, ALU.add)
                o.link(last)
                o.link(v.tensor_tensor(place, sums.rearrange("p e k -> p k e"), count, ALU.subtract))
                v.tensor_tensor(place, place, rank, ALU.add).then_inc(sem("ranks_read"), 1)
                beside(3)
                dve.wait_ge(sem("ranks_read"), r + 1)
                total = sums[:, :, GB - 1]
                if r < 2:
                    ti = n_tiles.bitcast(I32)
                    o.link(v.tensor_scalar(ti, total, float(P - 1), None, ALU.add))
                    o.link(v.tensor_scalar(ti, ti, P.bit_length() - 1, None, ALU.arith_shift_right))
                    o.link(v.tensor_copy(n_tiles, ti))
                    o.link(v.tensor_tensor_scan(taken, ones[:, 0:E8], n_tiles, 0.0, ALU.mult, ALU.add))
                    o.link(v.tensor_tensor(first_slot, taken, n_tiles, ALU.subtract))
                    o.link(v.tensor_scalar(first_slot, first_slot, float(P), None, ALU.mult))
                    owner = both.rearrange("p k e -> p (k e)")[:, 0:TILES0]
                    o.link(v.tensor_scalar(owner, tile_no, taken[:, 0:1], None, ALU.is_ge))
                    for e in range(1, E8 - 1):
                        o.link(v.scalar_tensor_tensor(out=owner, in0=tile_no, scalar=taken[:, e:e + 1], in1=owner,
                                                      op0=ALU.is_ge, op1=ALU.add))
                    o.link(v.tensor_copy(tile_expert[r].bitcast(I32), owner))
                    o.link(v.tensor_tensor(place, place, per_e(first_slot), ALU.add))
                    for k in range(2):
                        o.link(v.tensor_tensor(both, e_hot[:, k], place, ALU.mult))
                        o.link(v.tensor_reduce(pick, both, AX_X, ALU.add))
                        last = v.tensor_copy(slot[:, k, half].bitcast(I32), pick)
                        if k == 0:
                            o.link(last)
                        else:
                            last.then_inc(sem("slots_ready"), 1)
                else:
                    o.link(v.tensor_tensor(place, place, per_e(carry), ALU.add))
                    o.link(v.tensor_tensor(carry, carry, total, ALU.add))
                    dve.wait_ge(sem("weighed"), r + 1)
                    for k in range(2):
                        o.link(v.tensor_tensor(both, e_hot[:, k], place, ALU.mult))
                        o.link(v.tensor_reduce(pick, both, AX_X, ALU.add))
                        o.link(v.tensor_tensor(both, e_hot[:, k], per_e(cap_base), ALU.mult))
                        o.link(v.tensor_reduce(best, both, AX_X, ALU.add))
                        beside(4 + k)
                        o.link(v.tensor_tensor(best, best, pick, ALU.add))
                        o.link(v.tensor_scalar(pick, pick, float(CAP), None, ALU.is_ge))
                        o.link(v.scalar_tensor_tensor(out=best, in0=pick, scalar=float(NOWHERE), in1=best,
                                                      op0=ALU.mult, op1=ALU.add))
                        o.link(v.tensor_scalar(pick, pick, -1.0, 1.0, ALU.mult, ALU.add))
                        o.link(v.tensor_tensor(weight[:, k, half], weight[:, k, half], pick, ALU.mult))
                        last = v.tensor_copy(slot[:, k, half].bitcast(I32), best)
                        if k == 0:
                            o.link(last)
                        else:
                            last.then_inc(sem("slots_ready"), 1)
                dve.wait_ge(sem("slots_ready"), r + 1)
                route_links.append(o.base + o.k)

            def make_pieces(r, turn, u, odd=0):
                blk = bass.ds(GB * (r % 2) + 2 * turn + u, 1)
                first = 2 * u + 4 * odd
                for q in (first, first + 1):
                    before = sent(r, turn - odd, q)
                    if not (isinstance(before, int) and before == 0):
                        dve.wait_ge(sem(f"piece_out{q}"), 16 * before)
                rows, place = (piece, piece_slot) if not odd else (piece_more, more_slot)
                both = slice(2 * u, 2 * u + 2)
                v.tensor_scalar(rows[:, both, 0:P], xt[:, blk, :].to_broadcast([P, 2, P]),
                                ln_mean[:, blk], ln_rstd[:, blk], ALU.subtract, ALU.mult)
                v.tensor_copy(rows[:, both, P:P + 1].bitcast(I32), row_id[:, :, blk].bitcast(I32))
                v.tensor_copy(place[:, both].rearrange("p (k a) -> p k a", a=1).bitcast(I32), slot[:, :, blk].bitcast(I32)
                              ).then_inc(sem(f"pieces_made{u}"), 1)

            pipeline(dve, visit, route, aside)

            turns = TILES0 // RING

            def y_out_of(g, turn, q):
                T, u = g * TILES0 + RING * turn + q, q % 2
                dve.wait_ge(sem("y_done"), T + 1)
                dve.wait_ge(sem(f"y_out{q}"), 16 * (g * turns + turn))
                v.tensor_copy(y_tile[q], tp[1][:, 512 * u + F0:512 * u + F0 + P]).then_inc(sem("y_ready"), 1)

            def turn_tiles(g, turn, first, last, pieces, beside=None):
                te = tile_expert[g].bitcast(I32)
                for q in range(RING):
                    n, u = RING * turn + q, q % 2
                    T = g * TILES0 + n
                    e = dve.value_load(te[0:1, bass.ds(n, 1)], min_val=0, max_val=E8 - 1)
                    dve.wait_ge(sem("g_done"), T + 1)
                    if not (g == 0 and first and q < 2):
                        dve.wait_ge(sem("act_ready"), T - 1)
                    v.tensor_tensor(act_g[u], tp[1][:, 512 * u:512 * u + F0], b3_s[:, bass.ds(e * F0, F0)], ALU.add
                                    ).then_inc(sem("g_biased"), 1)
                    dve.wait_ge(sem("g_biased"), T + 1)
                    dve.wait_ge(sem("silu_ready"), T + 1)
                    v.tensor_tensor(act_h[u], act_h[u], act_g[u], ALU.mult).then_inc(sem("act_ready"), 1)
                    if not (first and q < 2):
                        y_out_of(g, turn if q >= 2 else turn - 1, (q - 2) % RING)
                    if pieces and q % 2:
                        make_pieces(1, RING // 4 * turn + q // 4, q // 2 % 2)
                    if beside is not None and q >= 2:
                        chunk_sum(*beside, q - 2)
                if last:
                    y_out_of(g, turn, q - 1)
                    y_out_of(g, turn, q)

            KC = KB // 2
            sums = [None, None]
            flat = lambda z: z.rearrange("p a c -> p (a c)")

            SUM_LINKS = 3 + STAT_LINKS + RSQRT_LINKS

            def add_expert(n, u, which, place):
                blocks = place[u].shape[1]
                for k in range(blocks):
                    at = flat(xt[:, bass.ds(blocks * n + k, 1), :])
                    last = v.scalar_tensor_tensor(out=at, in0=place[u][:, k, which, :],
                                                  scalar=weight[:, which, bass.ds(blocks * n + k, 1)],
                                                  in1=at, op0=ALU.mult, op1=ALU.add)
                return last

            def scales(o, mean, rstd, blocks, begin, end, chunks):
                last = rsqrt(v, o, var_c[:, 0:blocks], rsi_c[:, 0:blocks].bitcast(I32), rst_c[:, 0:blocks],
                             lambda t, y: v.scalar_tensor_tensor(out=rstd, in0=t, scalar=1.5, in1=y,
                                                                 op0=ALU.add, op1=ALU.mult),
                             begin=begin, end=end)
                if end:
                    o.link(last)
                    v.scalar_tensor_tensor(out=mean, in0=mean, scalar=-1.0, in1=rstd, op0=ALU.mult, op1=ALU.mult
                                           ).then_inc(sem("stats3"), chunks)
                    o.end()

            def chunk_sum(n, u, turn, part):
                o, blocks = sums[u], KC
                mean, rstd = mean_c[u][:, 0:blocks], rstd_c[u][:, 0:blocks]
                if part == 0:
                    o = sums[u] = Order(dve, sem("dve_sum"), n, SUM_LINKS)
                    dve.wait_ge(sem(f"y_in{u}"), 16 * (turn + 1))
                    o.step(add_expert(n, u, 0, y_in))
                elif part == 1:
                    o.settle()
                    add_expert(n, u, 1, y_in).then_inc(sem("x2_ready"), 1)
                elif part == 2:
                    dve.wait_ge(sem("x2_ready"), n + 1)
                    v.memset(idle[:, 0:1], 0.0)
                    for k in range(blocks):
                        last = v.bn_stats(st_c[:, k, :], xt[:, bass.ds(blocks * n + k, 1), :])
                    o.step(last)
                elif part == 3:
                    o.settle()
                    if not isinstance(n, int):
                        dve.wait_ge(sem("xn3_ready"), n - 1)
                    token_stats(v, o, st_c, mean, var_c[:, 0:blocks], rst_c[:, 0:blocks], 1e-6, blocks)
                else:
                    scales(o, mean, rstd, blocks, part == 4, part == 5, 1)

            turn_tiles(0, 0, True, False, True)
            with dve.Fori(1, 2 * GB // RING) as turn:
                turn_tiles(0, turn, False, False, True)
            for turn in range(2 * GB // RING, turns):
                turn_tiles(0, turn, False, turn == turns - 1, False)
            turn_tiles(1, 0, True, False, False, beside=(0, 0, 0))
            turn_tiles(1, 1, False, False, False, beside=(1, 1, 0))
            with dve.Fori(1, turns // 2) as turn:
                for u in range(2):
                    turn_tiles(1, 2 * turn + u, False, False, False, beside=(2 * turn + u, u, turn))
            turn_tiles(1, turns - 1, False, True, False)

            with dve.Fori(KB // 2, KB) as turn:
                o = Order(dve, sem("dve_sum"), turn - KB // 2, 4 + STAT_LINKS + RSQRT_LINKS, 2 * KB * SUM_LINKS)
                for u in range(2):
                    n = 2 * turn + u
                    dve.wait_ge(sem(f"y_in{u}"), 16 * (KB // 2 + turn + 1))
                    o.link(add_expert(n, u, 0, y_in8))
                    dve.wait_ge(sem("y_weighed"), n - KB + 1)
                    at = xt[:, bass.ds(KB * n, KB), :]
                    v.tensor_tensor(at, at, y_in8[u][:, :, 1, :], ALU.add).then_inc(sem("x2_ready"), 1)
                dve.wait_ge(sem("x2_ready"), KB + 2 * turn + 2)
                v.memset(idle[:, 0:1], 0.0)
                for k in range(2 * KB):
                    last = v.bn_stats(st_c[:, k, :], xt[:, bass.ds(2 * KB * turn + k, 1), :])
                o.link(last)
                dve.wait_ge(sem("xn3_ready"), KB + 2 * turn)
                token_stats(v, o, st_c, mean_2, var_c, rst_c, 1e-6, 2 * KB)
                scales(o, mean_2, rstd_2, 2 * KB, True, True, 2)

            dve.wait_ge(sem("biased"), NBLK // KB)
            with dve.Fori(0, NCG // 4) as turn:
                for n in range(8):
                    dve.wait_ge(sem("conv_done"), 8 * turn + n + 1)
                    for h in range(2):
                        half = slice(NBLK // 2 * h, NBLK // 2 * (h + 1))
                        other = slice(NBLK // 2 * (1 - h), NBLK // 2 * (2 - h))
                        at = xt[:, half, bass.ds(32 * turn + 4 * n, 4)]
                        last = v.tensor_tensor(at, at, banks[n].rearrange("p (c k) -> p k c", c=4)[:, other, :], ALU.add)
                    last.then_inc(sem("x3_ready"), 1)

            dve.wait_ge(sem("x3_ready"), C // 4)

            def take_logits(n, u):
                dve.wait_ge(sem("lg4_done"), n + 1)
                v.tensor_copy(logits[:, bass.ds(KB * n, KB), :], zp[u][:, 0:KB * E8].rearrange("p (k e) -> p k e", e=E8)
                              ).then_inc(sem("lg4_ready"), 1)

            def two_pieces(r, turn, odd):
                for u in range(2):
                    make_pieces(r, turn, u, odd)

            def router(turn, beside=False):
                rows = (lambda j: two_pieces(2, BESIDE * (turn - EARLY) + j, j % 2)) if beside else (lambda j: None)
                o = Order(dve, sem("dve_router"), turn, 2 + STAT_LINKS + RSQRT_LINKS)
                blks = bass.ds(2 * KB * turn, 2 * KB)
                for k in range(2 * KB):
                    last = v.bn_stats(st_r[:, k, :], xt[:, bass.ds(2 * KB * turn + k, 1), :])
                o.step(last)
                rows(0)
                o.settle()
                token_stats(v, o, st_r, ln_mean[:, blks], var_r, rst_r, 1e-5, 2 * KB)
                rows(1)
                last = rsqrt(v, o, var_r, rsi_r.bitcast(I32), rst_r,
                             lambda t, y: v.scalar_tensor_tensor(out=ln_rstd[:, blks], in0=t,
                                                                 scalar=1.5, in1=y, op0=ALU.add, op1=ALU.mult))
                o.link(last)
                v.memset(idle[:, 0:1], 0.0)
                v.scalar_tensor_tensor(out=ln_shift[:, blks], in0=ln_mean[:, blks], scalar=-1.0, in1=ln_rstd[:, blks],
                                       op0=ALU.mult, op1=ALU.mult).then_inc(sem("stats4"), 1)
                rows(2)
                for u in range(2):
                    n = 2 * turn + u
                    if not (isinstance(turn, int) and turn == 0):
                        dve.wait_ge(sem("tn4_done"), n - 1)
                    for k in range(DVE_SHARE):
                        blk = bass.ds(KB * n + k, 1)
                        last = v.tensor_scalar(tn4[u][:, k, :], flat(xt[:, blk, :]), ln_mean[:, blk], ln_rstd[:, blk],
                                               ALU.subtract, ALU.mult)
                    last.then_inc(sem("tn4_ready"), 1)
                if not (isinstance(turn, int) and turn == 0):
                    for u in range(2):
                        take_logits(2 * turn - 2 + u, u)
                rows(3)
                o.end()

            repeat(dve, 0, EARLY, router)
            route(2)
            router(EARLY, beside=True)
            with dve.Fori(EARLY + 1, NBLK // KB // 2) as turn:
                router(turn, beside=True)
            for u in range(2):
                take_logits(NBLK // KB - 2 + u, u)

            made = BESIDE * (NBLK // KB // 2 - EARLY)
            route(3, lambda j: two_pieces(2, made + j, j % 2))
            made += ROUTE_BESIDE
            for r, first in ((2, made // 2), (3, 0)):
                with dve.Fori(first, GB // 4) as turn:
                    for odd in range(2):
                        two_pieces(r, 2 * turn + odd, odd)

            per = CT // QT

            def last_bias(pair):
                for n in range(2 * per):
                    Q, u, s = 2 * per * pair + n, n % 2, n // per
                    dve.wait_ge(sem("yq_done"), Q + 1)
                    if n >= 2 or not isinstance(pair, int):
                        dve.wait_ge(sem(f"yq_out{(n - 2) % per}"), 64 * (2 * pair + (n - 2) // per + 1))
                    v.tensor_tensor(y_quad[u], zp[u][:, :].rearrange("p (q c) -> p q c", q=QT),
                                    fb2[s].rearrange("p (a c) -> p a c", a=1).to_broadcast([P, QT, P]), ALU.add
                                    ).then_inc(sem("yq_ready"), 1)

            repeat(dve, 0, E8 // 2, last_bias)

            def final_sum(turn, u):
                n = 2 * turn + u
                o = Order(dve, sem("dve_final"), n, 1)
                dve.wait_ge(sem(f"yf_in{u}"), 16 * (turn + 1))
                if not (isinstance(turn, int) and turn == 0):
                    dve.wait_ge(sem("fin_t_done"), n - 1)
                for k in range(KC):
                    last = v.scalar_tensor_tensor(out=fin[u][:, k, :], in0=y_fin[u][:, k, 0, :],
                                                  scalar=weight[:, 0, bass.ds(KC * n + k, 1)],
                                                  in1=flat(xt[:, bass.ds(KC * n + k, 1), :]), op0=ALU.mult, op1=ALU.add)
                o.link(last)
                for k in range(KC):
                    last = v.scalar_tensor_tensor(out=fin[u][:, k, :], in0=y_fin[u][:, k, 1, :],
                                                  scalar=weight[:, 1, bass.ds(KC * n + k, 1)],
                                                  in1=fin[u][:, k, :], op0=ALU.mult, op1=ALU.add)
                last.then_inc(sem("fin_ready"), 1)
                o.end()

            for u in range(2):
                final_sum(0, u)
            with dve.Fori(1, NBLK // 8) as turn:
                for u in range(2):
                    final_sum(turn, u)


_INS = ['x', 'L0_conv_se_w1', 'L0_conv_se_b1', 'L0_conv_se_w2', 'L0_conv_se_b2', 'L0_conv_down_w', 'L0_conv_gus',
        'L0_ffn_Wg', 'L0_ffn_W1', 'L0_ffn_W2', 'L0_ffn_W3', 'L0_ffn_b3', 'L1_conv_codebook', 'L1_conv_bias',
        'L1_ffn_gate_w', 'L1_ffn_w1', 'L1_ffn_b1', 'L1_ffn_w2', 'L1_ffn_b2']


def kernel(**inputs):
    import numpy as _np
    import concourse.bacc as _bacc
    from concourse import mybir as _mybir
    from concourse.bass_utils import run_bass_kernel_spmd as _run

    nc = _bacc.Bacc("TRN2", target_bir_lowering=False, num_devices=1)
    shapes = {'x': (B, C, HW), 'L0_conv_gus': (HW, HW)}
    arrays, args = {}, []
    for name in _INS:
        a = _np.ascontiguousarray(inputs[name])
        a = a.reshape(shapes.get(name, a.shape))
        arrays[f"in_{name}"] = a
        args.append(nc.dram_tensor(f"in_{name}", a.shape, _mybir.dt.from_np(a.dtype), kind="ExternalInput").ap())
    args.append(nc.dram_tensor("out", (B, C, HW), F32, kind="ExternalOutput").ap())
    metaformer(nc, *args)
    r = _run(nc, [arrays], core_ids=[0])
    return r.results[0]["out"].reshape(B, C, IMG, IMG)
```
